# Optimizing a Trainium2 kernel written in Bass

```python
import numpy as np
import jax
import jax.numpy as jnp

def _softmax(x, axis=-1):
    return jax.nn.softmax(x, axis=axis)

def _gelu(x):
    return jax.nn.gelu(x, approximate=True)

def _silu(x):
    return jax.nn.silu(x)

def _sigmoid(x):
    return jax.nn.sigmoid(x)

def _layernorm(x, axis=-1, eps=1e-05):
    m = jnp.mean(x, axis=axis, keepdims=True)
    v = jnp.var(x, axis=axis, keepdims=True)
    return (x - m) / jnp.sqrt(v + eps)

def _scatter_add(tgt, idx, src, axis=0):
    return tgt.at[idx].add(src)

def _segment_sum(src, seg, n):
    return jax.ops.segment_sum(src, seg, n)
kernel_name = 'mk_adj_preln_d2_adj_r2_b9e55c'

def setup_inputs(seed: int=0):
    np.random.seed(seed)
    _w = jnp.asarray

    def _rec_inputs():
        import jax
        import jax.numpy as jnp
        _gk = jax.random.key(seed)
        x = 0.0001732 + 1 * jax.random.normal(jax.random.fold_in(_gk, 1), (5120, 64), jnp.float32)
        _w = (1.0 + jnp.arange(5120, dtype=jnp.float32)) ** (-0.5)
        _w = _w / _w.mean()
        _pij = jnp.clip(0.00078125 * _w[:, None] * _w[None, :], 0.0, 1.0)
        _a = jax.random.uniform(jax.random.fold_in(_gk, 2), (5120, 5120)) < _pij
        _af = _a.astype(jnp.float32)
        _af = _af * jax.random.uniform(jax.random.fold_in(_gk, 3), (5120, 5120), jnp.float32, 0.05, 0.02)
        adj = _af
        return (x, adj)
    x, adj = _rec_inputs()

    def _L0_gnn_setup():
        import jax, jax.numpy as jnp
        import numpy as np
        N_USERS = 2048
        N_ITEMS = 3072
        EMB = 64
        LN_EPS = 1e-05
        key = jax.random.key(seed)
        ks = jax.random.split(key, 10)
        N = N_USERS + N_ITEMS
        ego = jax.random.normal(ks[0], (N, EMB), jnp.float32)
        adj = (jax.random.uniform(ks[1], (N, N), jnp.float32) < 0.01).astype(jnp.float32) * 0.02
        xav = float(np.sqrt(6.0 / (EMB + EMB)))
        W_u = jax.random.uniform(ks[2], (EMB, EMB), jnp.float32, -xav, xav)
        W_i = jax.random.uniform(ks[3], (EMB, EMB), jnp.float32, -xav, xav)
        diag_u = jax.random.uniform(ks[4], (N_USERS,), jnp.float32, 0.99, 1.01)
        diag_i = jax.random.uniform(ks[5], (N_ITEMS,), jnp.float32, 0.99, 1.01)
        par_u = jax.random.uniform(ks[6], (2,), jnp.float32, 0.0, 0.99)
        par_i = jax.random.uniform(ks[7], (2,), jnp.float32, 0.0, 0.99)
        ln_gamma = jnp.ones((EMB,), jnp.float32)
        ln_beta = jnp.zeros((EMB,), jnp.float32)
        return {'ego_embeddings': ego, 'adj': adj, 'W_u': W_u, 'diag_u': diag_u, 'par_u': par_u, 'W_i': W_i, 'diag_i': diag_i, 'par_i': par_i, 'ln_gamma': ln_gamma, 'ln_beta': ln_beta}
    _L0_gnn_all = _L0_gnn_setup()
    _L0_gnn_in = {k: v for k, v in _L0_gnn_all.items() if k in ('W_u', 'diag_u', 'par_u', 'W_i', 'diag_i', 'par_i', 'ln_gamma', 'ln_beta')}
    del _L0_gnn_all

    def _L1_gnn_setup():
        import jax, jax.numpy as jnp
        import numpy as np
        N = 8192
        F_IN = 64
        F_OUT = 64
        key = jax.random.key(seed)
        k1, k2, k3 = jax.random.split(key, 3)
        features = jax.random.normal(k1, (N, F_IN), dtype=jnp.float32)
        adj = jax.random.uniform(k2, (N, N), dtype=jnp.float32)
        W = jax.random.normal(k3, (F_OUT, 2 * F_IN), dtype=jnp.float32)
        return {'features': features, 'adj': adj, 'W': W}
    _L1_gnn_all = _L1_gnn_setup()
    _L1_gnn_in = {k: v for k, v in _L1_gnn_all.items() if k in ('W',)}
    del _L1_gnn_all
    return {'x': x, 'adj': adj, 'L0_gnn_W_u': _L0_gnn_in['W_u'], 'L0_gnn_diag_u': _L0_gnn_in['diag_u'], 'L0_gnn_par_u': _L0_gnn_in['par_u'], 'L0_gnn_W_i': _L0_gnn_in['W_i'], 'L0_gnn_diag_i': _L0_gnn_in['diag_i'], 'L0_gnn_par_i': _L0_gnn_in['par_i'], 'L0_gnn_ln_gamma': _L0_gnn_in['ln_gamma'], 'L0_gnn_ln_beta': _L0_gnn_in['ln_beta'], 'L1_gnn_W': _L1_gnn_in['W']}

def reference(x, adj, L0_gnn_W_u, L0_gnn_diag_u, L0_gnn_par_u, L0_gnn_W_i, L0_gnn_diag_i, L0_gnn_par_i, L0_gnn_ln_gamma, L0_gnn_ln_beta, L1_gnn_W):
    import jax
    import jax.numpy as jnp

    def _L0_gnn_ref(ego_embeddings, adj, W_u, diag_u, par_u, W_i, diag_i, par_i, ln_gamma, ln_beta):
        import jax, jax.numpy as jnp
        import numpy as np
        N_USERS = 2048
        N_ITEMS = 3072
        EMB = 64
        LN_EPS = 1e-05
        nu = diag_u.shape[0]
        res = ego_embeddings
        ego_u = ego_embeddings[:nu]
        ego_i = ego_embeddings[nu:]
        u = par_u[0] * par_u[1] * (diag_u[:, None] * ego_u @ W_u) + ego_u
        i = par_i[0] * par_i[1] * (diag_i[:, None] * ego_i @ W_i) + ego_i
        e = jnp.concatenate([u, i], axis=0)
        h = adj @ (adj.T @ e)
        mu = jnp.mean(h, axis=-1, keepdims=True)
        var = jnp.var(h, axis=-1, keepdims=True)
        out = (h - mu) * jax.lax.rsqrt(var + LN_EPS) * ln_gamma + ln_beta + res
        return out

    def _L1_gnn_ref(features, adj, W):
        import jax, jax.numpy as jnp
        import numpy as np
        N = 8192
        F_IN = 64
        F_OUT = 64
        neigh = jnp.matmul(adj, features)
        deg = jnp.sum(adj, axis=1, keepdims=True) + 1.0
        neigh = neigh / deg
        data = jnp.concatenate([features, neigh], axis=-1)
        return jnp.matmul(data, W.T)
    h = jnp.maximum(_layernorm(x, axis=-1), 0.0)
    x = x + _L0_gnn_ref(h, adj, L0_gnn_W_u, L0_gnn_diag_u, L0_gnn_par_u, L0_gnn_W_i, L0_gnn_diag_i, L0_gnn_par_i, L0_gnn_ln_gamma, L0_gnn_ln_beta)
    h = jnp.maximum(_layernorm(x, axis=-1), 0.0)
    x = x + _L1_gnn_ref(h, adj, L1_gnn_W)
    return x

_drawn_inputs = setup_inputs


def setup_inputs(seed=0):
    import zlib

    import numpy as np

    out = dict(_drawn_inputs(seed))
    spreads = {'L0_gnn_ln_gamma': (1.0, 0.2), 'L0_gnn_ln_beta': (0.0, 0.1)}
    factors = {'L0_gnn_diag_u': 8.0, 'L0_gnn_W_i': 3.483, 'L0_gnn_diag_i': 8.0}
    for name, (base, spread) in spreads.items():
        noise = np.random.default_rng([zlib.crc32(name.encode()), seed]).standard_normal(out[name].shape)
        drawn = base * np.exp(spread * noise) if base else spread * noise
        out[name] = jnp.asarray(drawn.astype(out[name].dtype))
    for name, factor in factors.items():
        out[name] = (out[name] * factor).astype(out[name].dtype)
    return out
```

```python
from contextlib import ExitStack

import concourse.bass as bass
from concourse import mybir

F32 = mybir.dt.float32
ALU = mybir.AluOpType
ACT = mybir.ActivationFunctionType
AX = mybir.AxisListType.X

P = 128
HALF = 64
BLK = 32
EPS = 1e-5


def gnn_kernel(nc, x, adj, w_u, diag_u, par_u, w_i, diag_i, par_i, gamma, beta, w_l1, out):
    N, E = x.shape
    N_USERS = diag_u.shape[0]
    assert E == HALF and w_l1.shape[0] == E
    TILES = N // P
    Q = 4
    GW = Q * P
    GROUPS = N // GW
    CW = 256
    CC = CW // P
    PANELS = N // CW
    NAT = 2 * GROUPS
    AT = 4
    BANKS = GROUPS // 2
    CHUNKS = TILES // 8
    CT = 8
    QUARTER = N // 4
    UW = 256
    UNITS = QUARTER // UW
    UC = UW // BLK
    IN_RING = NAT // Q
    ALL_UNITS = GROUPS * UNITS
    assert PANELS % 2 == 0 and UNITS == IN_RING and N_USERS % (CT * P) == 0

    with ExitStack() as ctx:
        def sb(name, shape):
            return ctx.enter_context(nc.sbuf_tensor(name, shape, F32))

        def bank(name):
            return ctx.enter_context(nc.psum_tensor(name, [P, 512], F32))

        def sem(name):
            return ctx.enter_context(nc.semaphore(name))

        nat = sb("nat", [P, NAT, Q, CW])
        unit_in = nat[:, :, :, :].rearrange("p (s a) q c -> p s (a q c)", s=IN_RING).rearrange(
            "p s (b c) -> p s b c", c=UW)
        unit_t = sb("unit_t", [P, 2, UC, GW])
        at = unit_t[:, 0, :, :].rearrange("p (s c) r -> p s c r", s=AT)
        xs = sb("xs", [P, TILES, E])
        h0 = sb("h0", [P, TILES, E])
        f_cols = h0
        res = sb("res", [P, TILES, E])
        e_sb = sb("e_sb", [P, TILES, E])
        f_sb = e_sb
        cen = sb("cen", [P, TILES, E])
        sq = sb("sq", [P, TILES, E])
        hT = sb("hT", [P, BANKS, GW])
        degp = sb("degp", [P, PANELS, TILES])
        rdeg = sb("rdeg", [P, TILES])
        h0T = sb("h0T", [P, Q, P])
        tT = sb("tT", [P, CW])
        t_sb = sb("t_sb", [P, 2, CC, E])
        ident = sb("ident", [P, P])
        fold = sb("fold", [P, E])
        center = sb("center", [P, P])
        zero_w = sb("zero_w", [P, E])
        w_user = sb("w_user", [P, P])
        w_item = sb("w_item", [P, P])
        wl = sb("wl", [E, 2 * E])
        wl_sw = sb("wl_sw", [E, 2 * E])
        w1T = sb("w1T", [P, P])
        w2T = sb("w2T", [P, E])
        diag = sb("diag", [TILES, P])
        par = sb("par", [P, 4])
        parp = sb("parp", [P, 2])
        scale = sb("scale", [P, TILES])
        gam = sb("gam", [P, E])
        bet = sb("bet", [P, E])
        s1 = sb("s1", [P, TILES])
        s2 = sb("s2", [P, TILES])
        rs = sb("rs", [P, TILES])
        sn = sb("sn", [P, TILES])
        stage = sb("stage", [P, 2, Q, E])
        fT = sb("fT", [P, 2, 2, P])
        nT = sb("nT", [P, 2, GW])
        o1 = sb("o1", [P, Q, E])
        o2 = sb("o2", [P, Q, E])
        obuf = sb("obuf", [P, 2, Q, E])

        H = [bank(f"H{b}") for b in range(BANKS)]
        TT = bank("TT")
        TA = [bank("TA0"), bank("TA1")]
        FIN = TT[:, CW:CW + CC * E].rearrange("p (c e) -> p c e", c=CC)

        x_full = [sem(f"x_full{c}") for c in range(CHUNKS)]
        const_full = sem("const_full")
        nat_full = [sem(f"nat_full{s}") for s in range(NAT)]
        unit_full = [sem(f"unit_full{s}") for s in range(IN_RING)]
        ident_step = sem("ident_step")
        zeros_ready = sem("zeros_ready")
        consts_ready = sem("consts_ready")
        dve_chain = sem("dve_chain")
        pool_chain = sem("pool_chain")
        const_t = sem("const_t")
        cen_ready = sem("cen_ready")
        sq_ready = sem("sq_ready")
        var_ready = sem("var_ready")
        std_ready = sem("std_ready")
        h0_ready = sem("h0_ready")
        h0T_psum = sem("h0T_psum")
        h0T_ready = sem("h0T_ready")
        hw_psum = sem("hw_psum")
        e_ready = sem("e_ready")
        res_ready = sem("res_ready")
        blocks_t = sem("blocks_t")
        at_full = sem("at_full")
        group_added = sem("group_added")
        tT_psum = sem("tT_psum")
        tT_ready = sem("tT_ready")
        t_psum = sem("t_psum")
        t_ready = sem("t_ready")
        deg_added = sem("deg_added")
        hT_ready = sem("hT_ready")
        hc_psum = sem("hc_psum")
        hsq_ready = sem("hsq_ready")
        hstd_ready = sem("hstd_ready")
        hvar_ready = sem("hvar_ready")
        c1_ready = sem("c1_ready")
        c1sq_ready = sem("c1sq_ready")
        c1var_ready = sem("c1var_ready")
        c1std_ready = sem("c1std_ready")
        f_ready = sem("f_ready")
        fcols_dve = sem("fcols_dve")
        fcols_act = sem("fcols_act")
        unit_t_full = sem("unit_t_full")
        unit_used = sem("unit_used")
        nT_ready = sem("nT_ready")
        stage_ready = sem("stage_ready")
        fT_psum = sem("fT_psum")
        fT_ready = sem("fT_ready")
        out_psum = sem("out_psum")
        o1_ready = sem("o1_ready")
        o2_ready = sem("o2_ready")
        obuf_ready = sem("obuf_ready")
        stored = [sem("stored0"), sem("stored1")]

        x_v = x.rearrange("(c p) e -> p c e", p=P)
        a_panel = adj.rearrange("(r q p) c -> r p q c", q=Q, p=P)
        a_unit = adj.rearrange("(b k) c -> k b c", k=BLK)
        out_v = out.rearrange("(c p) e -> p c e", p=P)

        def both(ap, n):
            return ap.unsqueeze(2).to_broadcast([P, n, E])

        def rows(ap, n):
            return ap.unsqueeze(1).to_broadcast([P, n, E])

        def tiles(k):
            return slice(CT * k, CT * k + CT)

        def slot(J_parity, R):
            return J_parity * GROUPS + R

        def unit_dma(eng, g, m_ring, col, blocks):
            return eng.dma_start(unit_in[BLK * g:BLK * g + BLK, m_ring, :, :],
                                 a_unit[:, blocks, bass.ds(col + g * QUARTER, UW)])

        block = ctx.enter_context(nc.Block())

        @block.sync
        def _(sp):
            for k in range(CHUNKS):
                sp.dma_start(xs[:, tiles(k), :], x_v[:, tiles(k), :]).then_inc(x_full[k], 16)
            for J in range(2):
                for R in range(GROUPS):
                    sp.dma_start(nat[:, slot(J, R), :, :],
                                 a_panel[R][:, :, J * CW:(J + 1) * CW]).then_inc(nat_full[slot(J, R)], 16)
            with sp.Fori(0, (PANELS - 2) // 2) as it:
                for u in range(2):
                    for R in range(GROUPS):
                        used = sp.snap(it * (2 * GROUPS * CC) + (u * GROUPS + R + 1) * CC)
                        sp.wait_ge(blocks_t, used)
                        sp.wait_ge(deg_added, used)
                        sp.dma_start(nat[:, slot(u, R), :, :],
                                     a_panel[R][:, :, bass.ds(it * (2 * CW) + (2 + u) * CW, CW)])\
                            .then_inc(nat_full[slot(u, R)], 16)
            for m in range(IN_RING):
                last = (PANELS - 2) * GROUPS + Q * m + Q - 1
                sp.wait_ge(blocks_t, CC * (last + 1))
                sp.wait_ge(deg_added, CC * (last + 1))
                for g in range(2):
                    unit_dma(sp, g, m, m * UW, slice(0, GW // BLK)).then_inc(unit_full[m], 16)
            with sp.Fori(1, GROUPS) as R:
                for v in range(UNITS):
                    sp.wait_ge(unit_t_full, R * (2 * UNITS) + (2 * (v + 1) - 2 * UNITS))
                    for g in range(2):
                        unit_dma(sp, g, v, v * UW, bass.ds(R * (GW // BLK), GW // BLK))\
                            .then_inc(unit_full[v], 16)
            for s in range(2):
                sp.wait_ge(stored[s], 16 * (GROUPS // 2))

        @block.gpsimd
        def _(pool):
            pool.memset(ident[:, :], 0.0).then_inc(ident_step, 1)
            pool.memset(zero_w[:, :], 0.0).then_inc(zeros_ready, 1)
            pool.memset(hT[:, 0, :], 0.0).then_inc(zeros_ready, 1)
            pool.memset(center[:, :], 0.0).then_inc(ident_step, 1)
            pool.wait_ge(ident_step, 2)
            pool.affine_select(out=ident[:, :], in_=ident[:, :], compare_op=ALU.not_equal, fill=1.0,
                               base=0, pattern=[[-1, P]], channel_multiplier=1).then_inc(ident_step, 1)
            pool.wait_ge(const_full, 16 * 14)
            for k in range(CHUNKS):
                pool.wait_ge(h0_ready, k + 1)
                pool.tensor_tensor(res[:, tiles(k), :], xs[:, tiles(k), :], h0[:, tiles(k), :], ALU.add)\
                    .then_inc(pool_chain, 1)
                pool.wait_ge(pool_chain, k + 1)
                pool.tensor_tensor(res[:, tiles(k), :], res[:, tiles(k), :], rows(bet[:, :], CT), ALU.add)\
                    .then_inc(res_ready, 1)
            pool.wait_ge(f_ready, CHUNKS)
            for u in range(2):
                pool.tensor_copy(stage[:, u, :, :], f_sb[:, Q * u:Q * u + Q, :]).then_inc(stage_ready, 1)

            def store(R, u):
                pool.wait_ge(obuf_ready, R + 1)
                t = slice(Q * R, Q * R + Q) if isinstance(R, int) else bass.ds(R * Q, Q)
                pool.dma_start(out_v[:, t, :], obuf[:, u, :, :]).then_inc(stored[u], 16)

            with pool.Fori(0, GROUPS // 2 - 1) as it:
                for u in range(2):
                    store(it * 2 + u, u)
                    pool.wait_ge(fT_psum, it * 2 + (u + 1))
                    pool.tensor_copy(stage[:, u, :, :], f_sb[:, bass.ds(it * (2 * Q) + (2 + u) * Q, Q), :])\
                        .then_inc(stage_ready, 1)
            for u in range(2):
                store(GROUPS - 2 + u, u)

        @block.tensor
        def _(pe):
            pe.wait_ge(ident_step, 3)
            pe.wait_ge(zeros_ready, 2)
            for R in range(GROUPS):
                a = HALF * (R % 2)
                pe.matmul(H[R // 2][a:a + HALF, :], zero_w[:, :], hT[:, 0, :], start=True, stop=False,
                          skip_group_check=True)
            pe.wait_ge(const_full, 16 * 14)
            pe.transpose(TA[0][:, 0:TILES], diag[:, :], ident[0:TILES, 0:TILES])
            pe.transpose(TA[0][:, 64:128], wl[:, :], ident[0:E, 0:E])
            pe.transpose(TA[0][:, 128:192], wl_sw[:, :], ident[0:E, 0:E]).then_inc(const_t, 1)
            pe.wait_ge(consts_ready, 1)
            for k in range(CHUNKS):
                pe.wait_ge(h0_ready, k + 1)
                if k:
                    pe.wait_ge(h0T_ready, k)
                for j in range(Q):
                    pair = h0[:, CT * k + 2 * j:CT * k + 2 * j + 2, :].rearrange("p t e -> p (t e)")
                    mm = pe.transpose(TA[0][:, j * P:(j + 1) * P], pair, ident[:, :])
                mm.then_inc(h0T_psum, 1)
                pe.wait_ge(h0T_ready, k + 1)
                if k:
                    pe.wait_ge(e_ready, k)
                w = w_user if CT * k * P < N_USERS else w_item
                for j in range(Q):
                    mm = pe.matmul(TA[1][:, j * P:(j + 1) * P], h0T[:, j, :], w[:, :], start=True, stop=True)
                mm.then_inc(hw_psum, 1)

            def transposes(n, parity, R):
                for c in range(CC):
                    if not (isinstance(n, int) and n == 0):
                        pe.wait_ge(at_full, (n - 1) * CC + (c + 1))
                    for q in range(Q):
                        mm = pe.transpose(TA[c][:, q * P:(q + 1) * P],
                                          nat[:, slot(parity, R), q, c * P:(c + 1) * P], ident[:, :])
                    mm.then_inc(blocks_t, 1)

            def add_group(n, J1, parity, R, last=False):
                pe.wait_ge(at_full, n * CC + CC)
                pe.wait_ge(t_ready, J1)
                a = HALF * (R % 2)
                for c in range(CC):
                    mm = pe.matmul(H[R // 2][a:a + HALF, :], t_sb[:, parity, c, :],
                                   at[:, (GROUPS * parity + R) % AT, c, :], start=False,
                                   stop=last and c == CC - 1, skip_group_check=True)
                mm.then_inc(group_added, 1)

            def panel(J, parity, loads, first=False, last=False):
                for R in range(GROUPS):
                    n = J * GROUPS + R
                    transposes(n, parity, R)
                    if R >= 2:
                        add_group(n - 2, J + 1, parity, R - 2, last)
                    elif not first:
                        add_group(n - 2, J, 1 - parity, GROUPS + R - 2)
                    if R == 0:
                        pe.wait_ge(tT_ready, J + 1)
                        for c in range(CC):
                            mm = pe.matmul(FIN[:, c, :], tT[:, c * P:(c + 1) * P], fold[:, :],
                                           start=True, stop=True)
                        mm.then_inc(t_psum, 1)
                    if not last:
                        if R == 1:
                            pe.wait_ge(t_ready, J + 1)
                        for r in ([R - 1] if R else []) + ([R] if R == GROUPS - 1 else []):
                            share(loads, 1 - parity, r)
                if last:
                    for R in (GROUPS - 2, GROUPS - 1):
                        add_group(J * GROUPS + R, J + 1, parity, R, last)

            def share(loads, parity, R):
                pe.wait_ge(nat_full[slot(parity, R)], loads)
                for q in range(Q):
                    a = HALF * (q % 2)
                    mm = pe.matmul(TT[a:a + HALF, 0:CW], e_sb[:, Q * R + q, :],
                                   nat[:, slot(parity, R), q, :], start=(R == 0 and q < 2),
                                   stop=(R == GROUPS - 1 and q >= Q - 2), skip_group_check=True)
                if R == GROUPS - 1:
                    mm.then_inc(tT_psum, 1)

            for R in range(GROUPS):
                if R % 2 == 0:
                    pe.wait_ge(e_ready, R // 2 + 1)
                share(16, 0, R)
            panel(0, 0, 16, first=True)
            with pe.Fori(0, (PANELS - 2) // 2) as it:
                panel(it * 2 + 1, 1, it * 16 + 32)
                panel(it * 2 + 2, 0, it * 16 + 32)
            panel(PANELS - 1, 1, 0, last=True)

            mid = [TA[0], TA[1], TT, H[0], H[1]]
            for b in range(BANKS):
                pe.wait_ge(hT_ready, b + 1)
                for q in range(Q):
                    mm = pe.matmul(mid[b][:, q * P:(q + 1) * P], hT[:, b, q * P:(q + 1) * P],
                                   center[:, :], start=True, stop=True)
                mm.then_inc(hc_psum, 1)

            def group_out_t(R1, u):
                pe.wait_ge(stage_ready, R1)
                if not (isinstance(R1, int) and R1 == 1):
                    pe.wait_ge(fT_ready, R1 - 1)
                for j in range(2):
                    mm = pe.transpose(TA[0][:, j * P:(j + 1) * P],
                                      stage[:, u, 2 * j:2 * j + 2, :].rearrange("p t e -> p (t e)"),
                                      ident[:, :])
                mm.then_inc(fT_psum, 1)

            def group_out(R1, u):
                pe.wait_ge(fT_ready, R1)
                pe.wait_ge(nT_ready, R1)
                if not (isinstance(R1, int) and R1 == 1):
                    pe.wait_ge(o2_ready, R1 - 1)
                for j in range(2):
                    pe.matmul(TA[1][:, j * P:(j + 1) * P], fT[:, u, j, :], w1T[:, :], start=True, stop=True)
                for q in range(Q):
                    mm = pe.matmul(TA[1][:, (Q + q) * E:(Q + q + 1) * E], nT[:, u, q * P:(q + 1) * P],
                                   w2T[:, :], start=True, stop=True)
                mm.then_inc(out_psum, 1)

            def group_b(R, u, first=False):
                for v in range(UNITS):
                    m = R * UNITS + v
                    pe.wait_ge(unit_t_full, m * 2 + 2)
                    if v == 0 and not first:
                        pe.wait_ge(nT_ready, R - 1)
                    for c in range(UC):
                        a = HALF * (c % 2)
                        mm = pe.matmul(H[u][a:a + HALF, :], f_cols[:, UC * v + c, :],
                                       unit_t[:, (UNITS * u + v) % 2, c, :], start=(v == 0 and c < 2),
                                       stop=(v == UNITS - 1 and c >= UC - 2), skip_group_check=True)
                    mm.then_inc(unit_used, 1)
                    if v == 1:
                        group_out_t(R + 1, u)
                    if v == 3 and not (isinstance(R, int) and R == 0):
                        group_out(R, 1 - u)

            pe.wait_ge(fcols_dve, 1)
            pe.wait_ge(fcols_act, 1)
            group_b(0, 0, first=True)
            group_b(1, 1, first=True)
            with pe.Fori(1, GROUPS // 2) as it:
                group_b(it * 2, 0)
                group_b(it * 2 + 1, 1)
            group_out(GROUPS, 1)

        @block.scalar
        def _(act):
            small = [(diag[0:N_USERS // P, :], diag_u.rearrange("(c p) -> c p", p=P)),
                     (diag[N_USERS // P:TILES, :], diag_i.rearrange("(c p) -> c p", p=P)),
                     (par[:, 0:2], par_u.partition_broadcast(P)), (par[:, 2:4], par_i.partition_broadcast(P)),
                     (gam[:, :], gamma.partition_broadcast(P)), (bet[:, :], beta.partition_broadcast(P)),
                     (w_user[0:E, 0:E], w_u), (w_user[E:P, E:P], w_u),
                     (w_item[0:E, 0:E], w_i), (w_item[E:P, E:P], w_i),
                     (wl[:, 0:E], w_l1[:, 0:E]), (wl[:, E:], w_l1[:, E:]),
                     (wl_sw[:, 0:E], w_l1[:, E:]), (wl_sw[:, E:], w_l1[:, 0:E])]
            assert len(small) == 14
            for dst, src in small:
                act.dma_start(dst, src).then_inc(const_full, 16)
            for k in range(CHUNKS):
                act.wait_ge(cen_ready, k + 1)
                act.activation(sq[:, tiles(k), :], cen[:, tiles(k), :], ACT.Square).then_inc(sq_ready, 1)
                act.wait_ge(var_ready, k + 1)
                act.activation(s2[:, tiles(k)], s1[:, tiles(k)], ACT.Sqrt).then_inc(std_ready, 1)
                act.wait_ge(h0T_psum, k + 1)
                if k:
                    act.wait_ge(hw_psum, k)
                act.copy(h0T[:, :, :], TA[0][:, :].rearrange("p (j r) -> p j r", j=Q)).then_inc(h0T_ready, 1)

            def to_sbuf(n, k, early=False):
                for c in range(CC):
                    act.wait_ge(blocks_t, n * CC + (c + 1))
                    if c == 0 and not early:
                        act.wait_ge(group_added, n - (AT - 1))
                    act.copy(at[:, k, c, :], TA[c][:, :]).then_inc(at_full, 1)

            for R in range(GROUPS):
                to_sbuf(R, R % AT, early=R < AT)
            with act.Fori(0, (PANELS - 2) // 2) as it:
                for n in range(GROUPS, 3 * GROUPS):
                    to_sbuf(it * (2 * GROUPS) + n, n % AT)
            base = (PANELS - 1) * GROUPS
            load_after = {0: [0], 1: [1], 3: [2], 7: [3], 9: [4]}
            for R in range(GROUPS):
                to_sbuf(base + R, (base + R) % AT)
                for m in load_after.get(R, []):
                    last = (PANELS - 2) * GROUPS + Q * m + Q - 1
                    act.wait_ge(blocks_t, CC * (last + 1))
                    act.wait_ge(deg_added, CC * (last + 1))
                    for g in range(2, 4):
                        unit_dma(act, g, m, m * UW, slice(0, GW // BLK)).then_inc(unit_full[m], 16)
            act.wait_ge(group_added, PANELS * GROUPS)
            for b in range(BANKS):
                act.copy(hT[:, b, :], H[b][:, :]).then_inc(hT_ready, 1)
            mid = [TA[0], TA[1], TT, H[0], H[1]]
            for b in range(BANKS):
                act.wait_ge(hc_psum, b + 1)
                act.activation(sq[:, tiles(b), :].rearrange("p (h q) e -> p q h e", h=2),
                               mid[b][:, :].rearrange("p (q h e) -> p q h e", q=Q, h=2),
                               ACT.Square).then_inc(hsq_ready, 1)
            act.wait_ge(hvar_ready, 1)
            act.activation(s2[:, :], s1[:, :], ACT.Sqrt).then_inc(hstd_ready, 1)
            for b in range(BANKS):
                act.wait_ge(c1_ready, b + 1)
                act.activation(sq[:, tiles(b), :], cen[:, tiles(b), :], ACT.Square).then_inc(c1sq_ready, 1)
            act.wait_ge(c1var_ready, 1)
            act.activation(s2[:, :], s1[:, :], ACT.Sqrt).then_inc(c1std_ready, 1)
            act.wait_ge(f_ready, CHUNKS)
            for g in range(1):
                for q in range(4):
                    cp = act.copy(f_cols[BLK * g:BLK * g + BLK, :, :].rearrange("p (a q) e -> p a q e", q=4)[:, :, q, :],
                                  f_sb[BLK * q:BLK * q + BLK, 10 * g:10 * g + 10, :])
            cp.then_inc(fcols_act, 1)

            def group_b(R, u, loads=True, first=False, last=False):
                for v in range(UNITS):
                    if loads:
                        act.wait_ge(unit_t_full, R * (2 * UNITS) + 2 * (v + 1))
                        for g in range(2, 4):
                            unit_dma(act, g, v, v * UW, bass.ds(R * (GW // BLK) + GW // BLK, GW // BLK))\
                                .then_inc(unit_full[v], 16)
                    if v == 2:
                        act.wait_ge(fT_psum, R + 1)
                        if not first:
                            act.wait_ge(out_psum, R - 1)
                        act.copy(fT[:, u, :, :], TA[0][:, 0:2 * P].rearrange("p (j r) -> p j r", j=2))\
                            .then_inc(fT_ready, 1)
                act.wait_ge(unit_used, R * UNITS + UNITS)
                act.copy(nT[:, u, :], H[u][:, :]).then_inc(nT_ready, 1)

            group_b(0, 0, first=True)
            group_b(1, 1, first=True)
            with act.Fori(1, GROUPS // 2 - 1) as it:
                group_b(it * 2, 0)
                group_b(it * 2 + 1, 1)
            group_b(GROUPS - 2, 0)
            group_b(GROUPS - 1, 1, loads=False)

        @block.vector
        def _(dve):
            chain = [0]

            def link(ins):
                chain[0] += 1
                ins.then_inc(dve_chain, 1)
                dve.wait_ge(dve_chain, chain[0])

            def inverse(t):
                link(dve.reciprocal(rs[:, t], s2[:, t]))
                link(dve.tensor_tensor(sn[:, t], rs[:, t], rs[:, t], ALU.mult))
                link(dve.tensor_tensor(sn[:, t], sn[:, t], s1[:, t], ALU.mult))
                link(dve.tensor_scalar(sn[:, t], sn[:, t], -0.5, 1.5, ALU.mult, ALU.add))
                link(dve.tensor_tensor(rs[:, t], rs[:, t], sn[:, t], ALU.mult))

            dve.wait_ge(ident_step, 3)
            for a in (0, HALF):
                link(dve.memset(center[a:a + HALF, a:a + HALF], -1.0 / E))
            for w in (w_user, w_item, w1T):
                dve.memset(w[0:E, E:P], 0.0)
                link(dve.memset(w[E:P, 0:E], 0.0))
            link(dve.tensor_tensor(center[:, :], center[:, :], ident[:, :], ALU.add))
            link(dve.tensor_tensor(fold[:, :], ident[:, 0:E], ident[:, E:P], ALU.add))

            def constants():
                dve.wait_ge(const_t, 1)
                dve.wait_ge(const_full, 16 * 14)
                link(dve.tensor_copy(w1T[0:E, 0:E], TA[0][0:E, 64:128]))
                link(dve.tensor_copy(w1T[E:P, E:P], TA[0][E:P, 128:192]))
                link(dve.tensor_copy(w2T[0:E, :], TA[0][0:E, 128:192]))
                link(dve.tensor_copy(w2T[E:P, :], TA[0][E:P, 64:128]))
                link(dve.tensor_tensor(parp[:, :], par[:, 0:4:2], par[:, 1:4:2], ALU.mult))
                NU = N_USERS // P
                link(dve.tensor_scalar(scale[:, 0:NU], TA[0][:, 0:NU], parp[:, 0:1], None, ALU.mult))
                dve.tensor_scalar(scale[:, NU:TILES], TA[0][:, NU:TILES], parp[:, 1:2], None, ALU.mult)\
                    .then_inc(consts_ready, 1)

            def normalize(k):
                t = tiles(k)
                dve.wait_ge(x_full[k], 16)
                link(dve.tensor_reduce(s1[:, t], xs[:, t, :], AX, ALU.add))
                link(dve.tensor_scalar(s1[:, t], s1[:, t], 1.0 / E, None, ALU.mult))
                dve.tensor_tensor(cen[:, t, :], xs[:, t, :], both(s1[:, t], CT), ALU.subtract)\
                    .then_inc(cen_ready, 1)
                dve.wait_ge(sq_ready, k + 1)
                link(dve.tensor_reduce(s1[:, t], sq[:, t, :], AX, ALU.add))
                dve.tensor_scalar(s1[:, t], s1[:, t], 1.0 / E, EPS, ALU.mult, ALU.add).then_inc(var_ready, 1)
                dve.wait_ge(std_ready, k + 1)
                inverse(t)
                dve.scalar_tensor_tensor(h0[:, t, :], cen[:, t, :], 0.0, both(rs[:, t], CT), ALU.max,
                                         ALU.mult).then_inc(h0_ready, 1)

            def embed(k):
                t = tiles(k)
                dve.wait_ge(hw_psum, k + 1)
                link(dve.tensor_tensor(e_sb[:, t, :], TA[1][:, :].rearrange("p (t e) -> p t e", t=CT),
                                       both(scale[:, t], CT), ALU.mult))
                dve.tensor_tensor(e_sb[:, t, :], e_sb[:, t, :], h0[:, t, :], ALU.add).then_inc(e_ready, 1)

            for k in range(CHUNKS):
                normalize(k)
                if k == 0:
                    constants()
                else:
                    embed(k - 1)
            embed(CHUNKS - 1)

            def panel(J, parity, loads):
                dve.wait_ge(tT_psum, J + 1)
                dve.tensor_copy(tT[:, :], TT[:, 0:CW]).then_inc(tT_ready, 1)
                dve.wait_ge(t_psum, J + 1)
                dve.tensor_copy(t_sb[:, parity, :, :], FIN).then_inc(t_ready, 1)
                for R in range(GROUPS):
                    dve.wait_ge(nat_full[slot(parity, R)], loads)
                    dve.tensor_reduce(degp[:, J, Q * R:Q * R + Q] if isinstance(J, int) else
                                      degp[:, bass.ds(J, 1), Q * R:Q * R + Q].rearrange("p j q -> p (j q)"),
                                      nat[:, slot(parity, R), :, :], AX, ALU.add).then_inc(deg_added, CC)

            with dve.Fori(0, PANELS // 2) as it:
                for u in range(2):
                    panel(it * 2 + u, u, it * 16 + 16)

            def transpose_unit(ring, k):
                for half in range(2):
                    b = slice(half * (GW // BLK // 2), (half + 1) * (GW // BLK // 2))
                    r = slice(half * (GW // 2), (half + 1) * (GW // 2))
                    dve.transpose(unit_t[:, k, :, r].rearrange("p c (b k) -> p b c k", k=BLK),
                                  unit_in[:, ring, b, :].rearrange("p b (c k) -> p b c k", k=BLK))\
                        .then_inc(unit_t_full, 1)

            dve.wait_ge(deg_added, CC * PANELS * GROUPS)
            link(dve.tensor_reduce(rdeg[:, :], degp[:, :, :].rearrange("p j c -> p c j"), AX, ALU.add))
            link(dve.tensor_scalar(rdeg[:, :], rdeg[:, :], 1.0, None, ALU.add))
            link(dve.reciprocal(rdeg[:, :], rdeg[:, :]))
            dve.wait_ge(group_added, PANELS * GROUPS)
            for m in range(2):
                dve.wait_ge(unit_full[m], 64)
                transpose_unit(m, m)

            mid = [TA[0], TA[1], TT, H[0], H[1]]
            for b in range(BANKS):
                dve.wait_ge(hsq_ready, b + 1)
                link(dve.tensor_reduce(s1[:, tiles(b)], sq[:, tiles(b), :], AX, ALU.add))
            dve.tensor_scalar(s1[:, :], s1[:, :], 1.0 / E, EPS, ALU.mult, ALU.add).then_inc(hvar_ready, 1)
            dve.wait_ge(hstd_ready, 1)
            inverse(slice(0, TILES))
            dve.wait_ge(res_ready, CHUNKS)
            for b in range(BANKS):
                t = tiles(b)
                for h in range(2):
                    th = slice(CT * b + Q * h, CT * b + Q * h + Q)
                    link(dve.tensor_tensor(cen[:, th, :], mid[b][:, :].rearrange("p (q h e) -> p h q e", q=Q, h=2)[:, h],
                                           both(rs[:, th], Q), ALU.mult))
                link(dve.tensor_tensor(cen[:, t, :], cen[:, t, :], rows(gam[:, :], CT), ALU.mult))
                link(dve.tensor_tensor(xs[:, t, :], cen[:, t, :], res[:, t, :], ALU.add))
                link(dve.tensor_reduce(s1[:, t], xs[:, t, :], AX, ALU.add))
            link(dve.tensor_scalar(s1[:, :], s1[:, :], 1.0 / E, None, ALU.mult))
            for b in range(BANKS):
                t = tiles(b)
                dve.tensor_tensor(cen[:, t, :], xs[:, t, :], both(s1[:, t], CT), ALU.subtract).then_inc(c1_ready, 1)
            for b in range(BANKS):
                t = tiles(b)
                dve.wait_ge(c1sq_ready, b + 1)
                link(dve.tensor_reduce(s1[:, t], sq[:, t, :], AX, ALU.add))
            dve.tensor_scalar(s1[:, :], s1[:, :], 1.0 / E, EPS, ALU.mult, ALU.add).then_inc(c1var_ready, 1)
            dve.wait_ge(c1std_ready, 1)
            inverse(slice(0, TILES))
            for b in range(BANKS):
                t = tiles(b)
                dve.scalar_tensor_tensor(f_sb[:, t, :], cen[:, t, :], 0.0, both(rs[:, t], CT), ALU.max,
                                         ALU.mult).then_inc(f_ready, 1)
            dve.wait_ge(f_ready, CHUNKS)
            for g in range(1, 4):
                for q in range(4):
                    cp = dve.tensor_copy(f_cols[BLK * g:BLK * g + BLK, :, :].rearrange("p (a q) e -> p a q e", q=4)[:, :, q, :],
                                         f_sb[BLK * q:BLK * q + BLK, 10 * g:10 * g + 10, :])
            cp.then_inc(fcols_dve, 1)

            def group_out(R1, R_half, u, first=False):
                cols = TA[1][:, :].rearrange("p (w q e) -> p w q e", q=Q, w=2)
                dve.wait_ge(out_psum, R1)
                if not (isinstance(R1, int) and R1 == 1):
                    dve.wait_ge(obuf_ready, R1 - 1)
                t = slice(Q * R1 - Q, Q * R1) if isinstance(R1, int) else bass.ds(R1 * Q - Q, Q)
                dve.tensor_tensor(o1[:, :, :], cols[:, 1, :, :], both(rdeg[:, t], Q), ALU.mult)\
                    .then_inc(o1_ready, 1)
                dve.tensor_tensor(o2[:, :, :], cols[:, 0, :, :], xs[:, t, :], ALU.add).then_inc(o2_ready, 1)
                dve.wait_ge(o1_ready, R1)
                dve.wait_ge(o2_ready, R1)
                if not first:
                    dve.wait_ge(stored[u], R_half * 16)
                dve.tensor_tensor(obuf[:, u, :, :], o1[:, :, :], o2[:, :, :], ALU.add).then_inc(obuf_ready, 1)

            def units_ahead(R, u, loads, n=UNITS):
                for w in range(2, 2 + n):
                    dve.wait_ge(unit_full[w % UNITS], loads + w // UNITS * 64)
                    dve.wait_ge(unit_used, R * UNITS + (w - 1))
                    transpose_unit(w % UNITS, (UNITS * u + w) % 2)

            units_ahead(0, 0, 64)
            units_ahead(1, 1, 128)
            group_out(1, 0, 0, first=True)
            units_ahead(2, 0, 192)
            group_out(2, 0, 1, first=True)
            with dve.Fori(1, GROUPS // 2 - 1) as it:
                units_ahead(it * 2 + 1, 1, it * 128 + 128)
                group_out(it * 2 + 1, it, 0)
                units_ahead(it * 2 + 2, 0, it * 128 + 192)
                group_out(it * 2 + 2, it, 1)
            units_ahead(GROUPS - 1, 1, 64 * GROUPS, n=UNITS - 2)
            group_out(GROUPS - 1, GROUPS // 2 - 1, 0)
            group_out(GROUPS, GROUPS // 2 - 1, 1)


_INS = ['x', 'adj', 'L0_gnn_W_u', 'L0_gnn_diag_u', 'L0_gnn_par_u', 'L0_gnn_W_i', 'L0_gnn_diag_i',
        'L0_gnn_par_i', 'L0_gnn_ln_gamma', 'L0_gnn_ln_beta', 'L1_gnn_W']
_OUTS = [((5120, 64), 'float32')]


def kernel(**inputs):
    import numpy as _np
    import concourse.bacc as _bacc
    from concourse import mybir as _mybir
    from concourse.bass_utils import run_bass_kernel_spmd as _run

    nc = _bacc.Bacc("TRN2", target_bir_lowering=False, num_devices=1)
    arrays, args = {}, []
    for name in _INS:
        a = _np.ascontiguousarray(inputs[name])
        arrays[f"in_{name}_dram"] = a
        args.append(nc.dram_tensor(f"in_{name}_dram", a.shape, _mybir.dt.from_np(a.dtype), kind="ExternalInput").ap())
    for i, (shape, dtype) in enumerate(_OUTS):
        dt = _mybir.dt.from_np(_np.dtype(dtype))
        args.append(nc.dram_tensor(f"out_{i}_dram", shape, dt, kind="ExternalOutput").ap())
    gnn_kernel(nc, *args)
    r = _run(nc, [arrays], core_ids=[0])
    got = tuple(r.results[0][f"out_{i}_dram"] for i in range(len(_OUTS)))
    return got[0]
```

```python
from contextlib import ExitStack

import concourse.bass as bass
from concourse import mybir

F32 = mybir.dt.float32
ALU = mybir.AluOpType
ACT = mybir.ActivationFunctionType
AX = mybir.AxisListType.X

P = 128
HALF = 64
BLK = 32
EPS = 1e-5


def gnn_kernel(nc, x, adj, w_u, diag_u, par_u, w_i, diag_i, par_i, gamma, beta, w_l1, out):
    N, E = x.shape
    N_USERS = diag_u.shape[0]
    assert E == HALF and w_l1.shape[0] == E
    TILES = N // P
    Q = 4
    GW = Q * P
    GROUPS = N // GW
    CW = 512
    CC = CW // P
    SW = CW // 4
    SUPER = N // (2 * CW)
    TURNS = GROUPS * CC + 1
    BANKS = GROUPS // 2
    CHUNKS = TILES // 8
    CT = 8
    QUARTER = N // 4
    UW = 256
    UNITS = QUARTER // UW
    UC = UW // BLK
    assert CC == Q and UNITS * 2 == GROUPS and CW == 2 * UW and N_USERS % (CT * P) == 0

    with ExitStack() as ctx:
        def sb(name, shape):
            return ctx.enter_context(nc.sbuf_tensor(name, shape, F32))

        def bank(name):
            return ctx.enter_context(nc.psum_tensor(name, [P, 512], F32))

        def sem(name):
            return ctx.enter_context(nc.semaphore(name))

        turned = sb("turned", [P, GROUPS, Q, CW])
        striped = sb("striped", [P, 2, Q, CW])
        unit_in = turned[:, :, :, :].rearrange("p (s a) q c -> p s (a q c)", s=UNITS).rearrange(
            "p s (b c) -> p s b c", c=UW)
        last_in = striped[:, :, :, :].rearrange("p a q c -> p (a q c)").rearrange(
            "p (b c) -> p b c", c=UW)
        unit_t = sb("unit_t", [P, 2, UC, GW])
        turned_t = unit_t[:, 0, :, :].rearrange("p (s c) r -> p s c r", s=2)
        strip_t = unit_t[:, 1, :, :].rearrange("p (s c) r -> p s c r", s=2)
        work = sb("work", [P, 3 * TILES * E])
        cen, sq, h0 = (work[:, i * TILES * E:(i + 1) * TILES * E].rearrange("p (t e) -> p t e", e=E)
                       for i in range(3))
        f_cols = h0
        strip_in = work[:, 0:2 * GW // BLK * SW].rearrange("p (s b c) -> p s b c", s=2, c=SW)
        xs = sb("xs", [P, TILES, E])
        res = sb("res", [P, TILES, E])
        e_sb = sb("e_sb", [P, TILES, E])
        f_sb = e_sb
        hT = sb("hT", [P, BANKS, GW])
        junk = hT[:, 1:5, :]
        degp = sb("degp", [P, 2 * SUPER, TILES])
        rdeg = sb("rdeg", [P, TILES])
        h0T = unit_t[:, 0, 0, :].rearrange("p (j r) -> p j r", j=Q)
        w_user = unit_t[:, 0, 1, 0:P]
        w_item = unit_t[:, 0, 1, P:2 * P]
        wl = unit_t[0:E, 0, 2, 0:2 * E]
        wl_sw = unit_t[0:E, 0, 2, 2 * E:4 * E]
        diag = unit_t[0:TILES, 0, 3, 0:P]
        tT = sb("tT", [P, CW])
        t_sb = sb("t_sb", [P, CC, 2, E])
        ident = sb("ident", [P, P])
        center = sb("center", [P, P])
        zero_w = sb("zero_w", [P, E])
        w1T = sb("w1T", [P, P])
        w2T = sb("w2T", [P, E])
        par = sb("par", [P, 4])
        parp = sb("parp", [P, 2])
        scale = sb("scale", [P, TILES])
        gam = sb("gam", [P, E])
        bet = sb("bet", [P, E])
        s1 = sb("s1", [P, TILES])
        s2 = sb("s2", [P, TILES])
        rs = sb("rs", [P, TILES])
        sn = sb("sn", [P, TILES])
        after = 0

        def place(n):
            nonlocal after
            after += n
            assert after <= 2 * TILES * E
            return work[:, after - n:after]

        stage = place(2 * Q * E).rearrange("p (u q e) -> p u q e", u=2, q=Q)
        fT = place(2 * 2 * P).rearrange("p (u j r) -> p u j r", u=2, j=2)
        nT = place(2 * GW).rearrange("p (u r) -> p u r", u=2)
        o1 = place(Q * E).rearrange("p (q e) -> p q e", q=Q)
        o2 = place(Q * E).rearrange("p (q e) -> p q e", q=Q)
        obuf = place(2 * Q * E).rearrange("p (u q e) -> p u q e", u=2, q=Q)

        H = [bank(f"H{b}") for b in range(BANKS)]
        TT = bank("TT")
        TA = [bank("TA0"), bank("TA1")]

        x_full = [sem(f"x_full{c}") for c in range(CHUNKS)]
        const_full = sem("const_full")
        turned_full = [sem(f"turned_full{R}") for R in range(GROUPS)]
        striped_full = [sem(f"striped_full{k}") for k in range(2)]
        strip_full = [sem(f"strip_full{k}") for k in range(2)]
        last_full = sem("last_full")
        unit_full = [sem(f"unit_full{s}") for s in range(UNITS)]
        ident_step = sem("ident_step")
        zeros_ready = sem("zeros_ready")
        zeros_used = sem("zeros_used")
        consts_ready = sem("consts_ready")
        dve_chain = sem("dve_chain")
        pool_chain = sem("pool_chain")
        const_t = sem("const_t")
        cen_ready = sem("cen_ready")
        sq_ready = sem("sq_ready")
        var_ready = sem("var_ready")
        std_ready = sem("std_ready")
        h0_ready = sem("h0_ready")
        h0T_psum = sem("h0T_psum")
        h0T_ready = sem("h0T_ready")
        hw_psum = sem("hw_psum")
        e_ready = sem("e_ready")
        res_ready = sem("res_ready")
        blocks_t = sem("blocks_t")
        t_psum = sem("t_psum")
        turn_full = sem("turn_full")
        turned_used = sem("turned_used")
        strip_t_full = sem("strip_t_full")
        strip_used = sem("strip_used")
        shared = sem("shared")
        tT_ready = sem("tT_ready")
        deg_turned = sem("deg_turned")
        deg_striped = sem("deg_striped")
        sum_ready = sem("sum_ready")
        hT_ready = sem("hT_ready")
        hc_psum = sem("hc_psum")
        hsq_ready = sem("hsq_ready")
        hstd_ready = sem("hstd_ready")
        hvar_ready = sem("hvar_ready")
        c1_ready = sem("c1_ready")
        c1sq_ready = sem("c1sq_ready")
        c1var_ready = sem("c1var_ready")
        c1std_ready = sem("c1std_ready")
        f_ready = sem("f_ready")
        fcols_dve = sem("fcols_dve")
        fcols_act = sem("fcols_act")
        unit_t_full = sem("unit_t_full")
        unit_used = sem("unit_used")
        nT_ready = sem("nT_ready")
        stage_ready = sem("stage_ready")
        fT_psum = sem("fT_psum")
        fT_ready = sem("fT_ready")
        out_psum = sem("out_psum")
        o1_ready = sem("o1_ready")
        o2_ready = sem("o2_ready")
        obuf_ready = sem("obuf_ready")
        stored = [sem("stored0"), sem("stored1")]

        x_v = x.rearrange("(c p) e -> p c e", p=P)
        a_panel = adj.rearrange("(r q p) c -> r p q c", q=Q, p=P)
        a_strip = adj.rearrange("(b k) c -> k b c", k=BLK)
        out_v = out.rearrange("(c p) e -> p c e", p=P)

        def both(ap, n):
            return ap.unsqueeze(2).to_broadcast([P, n, E])

        def rows(ap, n):
            return ap.unsqueeze(1).to_broadcast([P, n, E])

        def tiles(k):
            return slice(CT * k, CT * k + CT)

        def strips(eng, g, dst, col, quarter, blocks):
            w = dst.shape[2]
            cols = slice(col + g * quarter, col + g * quarter + w) if isinstance(col, int) \
                else bass.ds(col + g * quarter, w)
            return eng.dma_start(dst[BLK * g:BLK * g + BLK, :, :], a_strip[:, blocks, cols])

        def group_blocks(R):
            n = GW // BLK
            return slice(n * R, n * R + n) if isinstance(R, int) else bass.ds(R * n, n)

        def turn(R, c):
            return R * CC + c + (1 if R or c >= 2 else 0)

        block = ctx.enter_context(nc.Block())

        @block.sync
        def _(sp):
            for k in range(CHUNKS):
                sp.dma_start(xs[:, tiles(k), :], x_v[:, tiles(k), :]).then_inc(x_full[k], 16)

            def load_turned(R, col):
                sp.dma_start(turned[:, R, :, :], a_panel[R][:, :, col]).then_inc(turned_full[R], 16)

            def load_striped(R, col):
                sp.dma_start(striped[:, R % 2, :, :], a_panel[R][:, :, col]).then_inc(striped_full[R % 2], 16)

            order = [2, 3, 5, 6, 7, 8, 9, 10, 10, 10]
            for R in range(GROUPS):
                for r in range(order[R - 1] if R else 0, order[R]):
                    if r < GROUPS:
                        load_turned(r, slice(0, CW))
                if R >= 2:
                    sp.wait_ge(shared, Q * (R - 1))
                    sp.wait_ge(deg_striped, Q * (R - 1))
                load_striped(R, slice(CW, 2 * CW))
                if R == 6:
                    sp.wait_ge(h0_ready, CHUNKS)
                    for g in range(2):
                        strips(sp, g, strip_in[:, 0, :, :], CW, SW, group_blocks(0)).then_inc(strip_full[0], 16)

            with sp.Fori(0, SUPER - 1) as i:
                for R in range(GROUPS):
                    before = sp.snap(i * TILES + Q * (GROUPS + R - 1))
                    col = sp.snap(i * (2 * CW) + 3 * CW)
                    sp.wait_ge(shared, before)
                    sp.wait_ge(deg_striped, before)
                    load_striped(R, bass.ds(col, CW))
                    read = sp.snap(i * TILES + Q * (R + 1))
                    col = sp.snap(i * (2 * CW) + 2 * CW)
                    sp.wait_ge(blocks_t, read)
                    sp.wait_ge(deg_turned, read)
                    load_turned(R, bass.ds(col, CW))
                    if R:
                        free = sp.snap(i * GROUPS + R)
                    cols = [sp.snap(i * (2 * CW) + ((CW if R < GROUPS - 1 else 3 * CW) + g * SW)) for g in range(2)]
                    if R:
                        sp.wait_ge(strip_t_full, free)
                    for g in range(2):
                        strips(sp, g, strip_in[:, (R + 1) % 2, :, :], cols[g], 0, group_blocks((R + 1) % GROUPS))\
                            .then_inc(strip_full[(R + 1) % 2], 16)
            sp.wait_ge(shared, SUPER * TILES)
            sp.wait_ge(deg_striped, SUPER * TILES)
            sp.wait_ge(deg_turned, SUPER * TILES)
            for R in range(GROUPS):
                if R < GROUPS - 1:
                    sp.wait_ge(strip_t_full, (SUPER - 1) * GROUPS + R)
                    for g in range(2):
                        strips(sp, g, strip_in[:, (R + 1) % 2, :, :], (2 * SUPER - 1) * CW, SW,
                               group_blocks(R + 1)).then_inc(strip_full[(R + 1) % 2], 16)
                if R == 0:
                    for g in range(2):
                        strips(sp, g, last_in, (UNITS - 1) * UW, QUARTER, group_blocks(GROUPS - 1))\
                            .then_inc(last_full, 16)
                if R % 2:
                    m = R // 2
                    sp.wait_ge(blocks_t, (SUPER - 1) * TILES + Q * (R + 1))
                    for g in range(2):
                        strips(sp, g, unit_in[:, m, :, :], m * UW, QUARTER, group_blocks(0))\
                            .then_inc(unit_full[m], 16)

            def load_units(R, n=UNITS):
                for v in range(n):
                    sp.wait_ge(unit_t_full, R * (2 * UNITS) + (2 * (v + 1) - 2 * UNITS))
                    for g in range(2):
                        strips(sp, g, unit_in[:, v, :, :], v * UW, QUARTER, group_blocks(R))\
                            .then_inc(unit_full[v], 16)

            with sp.Fori(1, GROUPS - 1) as R:
                load_units(R)
            load_units(GROUPS - 1, UNITS - 1)
            for s in range(2):
                sp.wait_ge(stored[s], 16 * (GROUPS // 2))

        @block.gpsimd
        def _(pool):
            pool.memset(ident[:, :], 0.0).then_inc(ident_step, 1)
            pool.memset(zero_w[:, :], 0.0).then_inc(zeros_ready, 1)
            pool.memset(hT[:, 0, :], 0.0).then_inc(zeros_ready, 1)
            pool.memset(center[:, :], 0.0).then_inc(ident_step, 1)
            pool.wait_ge(ident_step, 2)
            pool.affine_select(out=ident[:, :], in_=ident[:, :], compare_op=ALU.not_equal, fill=1.0,
                               base=0, pattern=[[-1, P]], channel_multiplier=1).then_inc(ident_step, 1)
            pool.wait_ge(const_full, 16 * 14)
            for k in range(CHUNKS):
                pool.wait_ge(h0_ready, k + 1)
                pool.tensor_tensor(res[:, tiles(k), :], xs[:, tiles(k), :], h0[:, tiles(k), :], ALU.add)\
                    .then_inc(pool_chain, 1)
                pool.wait_ge(pool_chain, k + 1)
                pool.tensor_tensor(res[:, tiles(k), :], res[:, tiles(k), :], rows(bet[:, :], CT), ALU.add)\
                    .then_inc(res_ready, 1)
            pool.wait_ge(f_ready, CHUNKS)
            for u in range(2):
                pool.tensor_copy(stage[:, u, :, :], f_sb[:, Q * u:Q * u + Q, :]).then_inc(stage_ready, 1)

            def store(R, u):
                pool.wait_ge(obuf_ready, R + 1)
                t = slice(Q * R, Q * R + Q) if isinstance(R, int) else bass.ds(R * Q, Q)
                pool.dma_start(out_v[:, t, :], obuf[:, u, :, :]).then_inc(stored[u], 16)

            with pool.Fori(0, GROUPS // 2 - 1) as it:
                for u in range(2):
                    store(it * 2 + u, u)
                    pool.wait_ge(fT_psum, it * 2 + (u + 1))
                    pool.tensor_copy(stage[:, u, :, :], f_sb[:, bass.ds(it * (2 * Q) + (2 + u) * Q, Q), :])\
                        .then_inc(stage_ready, 1)
            for u in range(2):
                store(GROUPS - 2 + u, u)

        @block.tensor
        def _(pe):
            pe.wait_ge(ident_step, 3)
            pe.wait_ge(zeros_ready, 2)
            for R in range(GROUPS):
                a = HALF * (R % 2)
                mm = pe.matmul(H[R // 2][a:a + HALF, :], zero_w[:, :], hT[:, 0, :], start=True, stop=False,
                               skip_group_check=True)
            mm.then_inc(zeros_used, 1)
            pe.wait_ge(const_full, 16 * 14)
            pe.transpose(TA[0][:, 0:TILES], diag[:, :], ident[0:TILES, 0:TILES])
            pe.transpose(TA[0][:, 64:128], wl[:, :], ident[0:E, 0:E])
            pe.transpose(TA[0][:, 128:192], wl_sw[:, :], ident[0:E, 0:E]).then_inc(const_t, 1)
            pe.wait_ge(consts_ready, 1)
            for k in range(CHUNKS):
                pe.wait_ge(h0_ready, k + 1)
                if k:
                    pe.wait_ge(h0T_ready, k)
                for j in range(Q):
                    pair = h0[:, CT * k + 2 * j:CT * k + 2 * j + 2, :].rearrange("p t e -> p (t e)")
                    mm = pe.transpose(TA[0][:, j * P:(j + 1) * P], pair, ident[:, :])
                mm.then_inc(h0T_psum, 1)
                pe.wait_ge(h0T_ready, k + 1)
                if k:
                    pe.wait_ge(e_ready, k)
                w = w_user if CT * k * P < N_USERS else w_item
                for j in range(Q):
                    mm = pe.matmul(TA[1][:, j * P:(j + 1) * P], h0T[:, j, :], w[:, :], start=True, stop=True)
                mm.then_inc(hw_psum, 1)

            def share_turned(R, q):
                return pe.matmul(TT[0:HALF, :], e_sb[:, Q * R + q, :], turned[:, R, q, :],
                                 start=(R == 0 and q == 0), stop=(R == GROUPS - 1 and q == Q - 1),
                                 skip_group_check=True)

            def share_striped(R, q):
                return pe.matmul(TT[HALF:P, :], e_sb[:, Q * R + q, :], striped[:, R % 2, q, :],
                                 start=(R == 0 and q == 0), stop=(R == GROUPS - 1 and q == Q - 1),
                                 skip_group_check=True)

            def wait_loads(i1, R):
                pe.wait_ge(turned_full[R], i1 * 16)
                pe.wait_ge(striped_full[R % 2], (i1 - 1) * (16 * UNITS) + (16 * (R // 2) + 16))

            def share(i1, R):
                wait_loads(i1, R)
                for q in range(Q):
                    share_turned(R, q)
                    mm = share_striped(R, q)
                mm.then_inc(shared, Q)

            def turn_blocks(i, R, c):
                k = turn(R, c)
                if k >= 2:
                    pe.wait_ge(turn_full, i * TURNS + (k - 1))
                for q in range(Q):
                    mm = pe.transpose(TA[k % 2][:, q * P:(q + 1) * P],
                                      turned[:, R, q, c * P:(c + 1) * P], ident[:, :])
                mm.then_inc(blocks_t, 1)

            def add_turned(R, c):
                a = HALF * (R % 2)
                mm = pe.matmul(H[R // 2][a:a + HALF, :], t_sb[:, c, 0, :], turned_t[:, R % 2, c, :],
                               start=False, stop=False, skip_group_check=True)
                if c == CC - 1:
                    mm.then_inc(turned_used, 1)

            def add_strip(R, c, last):
                a = HALF * (R % 2)
                mm = pe.matmul(H[R // 2][a:a + HALF, :], t_sb[:, c, 1, :], strip_t[:, R % 2, c, :],
                               start=False, stop=last and c == CC - 1, skip_group_check=True)
                if c == CC - 1:
                    mm.then_inc(sum_ready if last and R == GROUPS - 1 else strip_used, 1)

            def superpanel(i, last=False):
                for R in range(GROUPS):
                    turn_blocks(i, R, 0)
                    turn_blocks(i, R, 1)
                    if R == 0:
                        pe.wait_ge(tT_ready, i * 2 + 2)
                        pe.wait_ge(turn_full, i * TURNS + 1)
                        for c in range(CC):
                            mm = pe.transpose(TA[0][:, c * P:(c + 1) * P], tT[:, c * P:(c + 1) * P],
                                              ident[:, :])
                        mm.then_inc(t_psum, 1)
                    else:
                        pe.wait_ge(turn_full, i * TURNS + (turn(R - 1, CC - 1) + 1))
                        if R > 1:
                            pe.wait_ge(strip_t_full, i * GROUPS + (R - 1))
                        for c in range(CC):
                            add_turned(R - 1, c)
                            if R > 1:
                                add_strip(R - 2, c, last)
                    turn_blocks(i, R, 2)
                    turn_blocks(i, R, 3)
                    if R and not last:
                        share(i + 2, R - 1)
                pe.wait_ge(turn_full, i * TURNS + TURNS)
                pe.wait_ge(strip_t_full, i * GROUPS + (GROUPS - 1))
                for c in range(CC):
                    add_turned(GROUPS - 1, c)
                    add_strip(GROUPS - 2, c, last)
                pe.wait_ge(strip_t_full, i * GROUPS + GROUPS)
                if last:
                    for c in range(CC):
                        add_strip(GROUPS - 1, c, last)
                else:
                    wait_loads(i + 2, GROUPS - 1)
                    for c in range(CC):
                        add_strip(GROUPS - 1, c, last)
                        share_turned(GROUPS - 1, c)
                    for q in range(Q):
                        mm = share_striped(GROUPS - 1, q)
                    mm.then_inc(shared, Q)

            for R in range(GROUPS):
                if R % 2 == 0:
                    pe.wait_ge(e_ready, R // 2 + 1)
                share(1, R)
            with pe.Fori(0, SUPER - 1) as i:
                superpanel(i)
            superpanel(SUPER - 1, last=True)

            mid = [TA[0], TA[1], TT, H[0], H[1]]
            for b in range(BANKS):
                pe.wait_ge(hT_ready, b + 1)
                for q in range(Q):
                    mm = pe.matmul(mid[b][:, q * P:(q + 1) * P], hT[:, b, q * P:(q + 1) * P],
                                   center[:, :], start=True, stop=True)
                mm.then_inc(hc_psum, 1)

            def group_out_t(R1, u):
                pe.wait_ge(stage_ready, R1)
                if not (isinstance(R1, int) and R1 == 1):
                    pe.wait_ge(fT_ready, R1 - 1)
                for j in range(2):
                    mm = pe.transpose(TA[0][:, j * P:(j + 1) * P],
                                      stage[:, u, 2 * j:2 * j + 2, :].rearrange("p t e -> p (t e)"),
                                      ident[:, :])
                mm.then_inc(fT_psum, 1)

            def group_out(R1, u):
                pe.wait_ge(fT_ready, R1)
                pe.wait_ge(nT_ready, R1)
                if not (isinstance(R1, int) and R1 == 1):
                    pe.wait_ge(o2_ready, R1 - 1)
                for j in range(2):
                    pe.matmul(TA[1][:, j * P:(j + 1) * P], fT[:, u, j, :], w1T[:, :], start=True, stop=True)
                for q in range(Q):
                    mm = pe.matmul(TA[1][:, (Q + q) * E:(Q + q + 1) * E], nT[:, u, q * P:(q + 1) * P],
                                   w2T[:, :], start=True, stop=True)
                mm.then_inc(out_psum, 1)

            def group_b(R, u, first=False):
                for v in range(UNITS):
                    m = R * UNITS + v
                    pe.wait_ge(unit_t_full, m * 2 + 2)
                    if v == 0 and not first:
                        pe.wait_ge(nT_ready, R - 1)
                    for c in range(UC):
                        a = HALF * (c % 2)
                        mm = pe.matmul(H[u][a:a + HALF, :], f_cols[:, UC * v + c, :],
                                       unit_t[:, (UNITS * u + v) % 2, c, :], start=(v == 0 and c < 2),
                                       stop=(v == UNITS - 1 and c >= UC - 2), skip_group_check=True)
                    mm.then_inc(unit_used, 1)
                    if v == 1:
                        group_out_t(R + 1, u)
                    if v == 3 and not (isinstance(R, int) and R == 0):
                        group_out(R, 1 - u)

            pe.wait_ge(fcols_dve, 1)
            pe.wait_ge(fcols_act, 1)
            group_b(0, 0, first=True)
            group_b(1, 1, first=True)
            with pe.Fori(1, GROUPS // 2) as it:
                group_b(it * 2, 0)
                group_b(it * 2 + 1, 1)
            group_out(GROUPS, 1)

        @block.scalar
        def _(act):
            small = [(diag[0:N_USERS // P, :], diag_u.rearrange("(c p) -> c p", p=P)),
                     (diag[N_USERS // P:TILES, :], diag_i.rearrange("(c p) -> c p", p=P)),
                     (par[:, 0:2], par_u.partition_broadcast(P)), (par[:, 2:4], par_i.partition_broadcast(P)),
                     (gam[:, :], gamma.partition_broadcast(P)), (bet[:, :], beta.partition_broadcast(P)),
                     (w_user[0:E, 0:E], w_u), (w_user[E:P, E:P], w_u),
                     (w_item[0:E, 0:E], w_i), (w_item[E:P, E:P], w_i),
                     (wl[:, 0:E], w_l1[:, 0:E]), (wl[:, E:], w_l1[:, E:]),
                     (wl_sw[:, 0:E], w_l1[:, E:]), (wl_sw[:, E:], w_l1[:, 0:E])]
            assert len(small) == 14
            for dst, src in small:
                act.dma_start(dst, src).then_inc(const_full, 16)
            for k in range(CHUNKS):
                act.wait_ge(cen_ready, k + 1)
                act.activation(sq[:, tiles(k), :], cen[:, tiles(k), :], ACT.Square).then_inc(sq_ready, 1)
                act.wait_ge(var_ready, k + 1)
                act.activation(s2[:, tiles(k)], s1[:, tiles(k)], ACT.Sqrt).then_inc(std_ready, 1)
                act.wait_ge(h0T_psum, k + 1)
                if k:
                    act.wait_ge(hw_psum, k)
                act.copy(h0T[:, :, :], TA[0][:, :].rearrange("p (j r) -> p j r", j=Q)).then_inc(h0T_ready, 1)

            def degrees(i2, R, q0, n, first=False):
                for q in range(q0, q0 + n):
                    if not first or R:
                        act.wait_ge(deg_striped, Q * R + q - (Q - 1) if first else i2 * (TILES // 2) + (Q * R + q - (Q - 1)))
                    place = degp[:, i2 + 1, Q * R + q:Q * R + q + 1] if isinstance(i2, int) else \
                        degp[:, bass.ds(i2 + 1, 1), Q * R + q:Q * R + q + 1].rearrange("p a b -> p (a b)")
                    act.activation(junk[:, q, :], striped[:, R % 2, q, :], ACT.Copy, accum_out=place)\
                        .then_inc(deg_striped, 1)

            def to_sbuf(i, R, c):
                k = turn(R, c)
                act.wait_ge(blocks_t, i * TILES + (CC * R + c + 1))
                if c == 0 and R >= 2:
                    act.wait_ge(turned_used, i * GROUPS + (R - 1))
                act.copy(turned_t[:, R % 2, c, :], TA[k % 2][:, :]).then_inc(turn_full, 1)

            def superpanel(i, last=False):
                act.wait_ge(shared, i * TILES + TILES)
                act.copy(tT[0:HALF, :], TT[0:HALF, :]).then_inc(tT_ready, 1)
                act.copy(tT[HALF:P, :].rearrange("p (c g k) -> p g c k", g=4, c=CC),
                         TT[HALF:P, :].rearrange("p (g c k) -> p g c k", g=4, c=CC)).then_inc(tT_ready, 1)
                for R in range(GROUPS):
                    to_sbuf(i, R, 0)
                    to_sbuf(i, R, 1)
                    if R == 0:
                        act.wait_ge(t_psum, i + 1)
                        act.copy(t_sb[:, :, :, :], TA[0][:, :].rearrange("p (c w e) -> p c w e", c=CC, w=2))\
                            .then_inc(turn_full, 1)
                    elif not last:
                        act.wait_ge(striped_full[(R - 1) % 2], i * (16 * UNITS) + (16 * UNITS + 16 * ((R - 1) // 2) + 16))
                        degrees(i * 2 + 2, R - 1, 0, 2)
                    to_sbuf(i, R, 2)
                    to_sbuf(i, R, 3)
                    if R and not last:
                        degrees(i * 2 + 2, R - 1, 2, 2)
                    if not (last and R == GROUPS - 1):
                        if R:
                            act.wait_ge(strip_t_full, i * GROUPS + R)
                        for g in range(2, 4):
                            strips(act, g, strip_in[:, (R + 1) % 2, :, :],
                                   i * (2 * CW) + (CW if R < GROUPS - 1 else 3 * CW), SW,
                                   group_blocks((R + 1) % GROUPS)).then_inc(strip_full[(R + 1) % 2], 16)
                    if last and R == 0:
                        act.wait_ge(shared, SUPER * TILES)
                        act.wait_ge(deg_striped, SUPER * TILES)
                        for g in range(2, 4):
                            strips(act, g, last_in, (UNITS - 1) * UW, QUARTER, group_blocks(GROUPS - 1))\
                                .then_inc(last_full, 16)
                    if last and R % 2:
                        act.wait_ge(blocks_t, i * TILES + CC * (R + 1))
                        act.wait_ge(deg_turned, SUPER * TILES)
                        for g in range(2, 4):
                            strips(act, g, unit_in[:, R // 2, :, :], R // 2 * UW, QUARTER, group_blocks(0))\
                                .then_inc(unit_full[R // 2], 16)
                if not last:
                    act.wait_ge(striped_full[(GROUPS - 1) % 2], i * (16 * UNITS) + 2 * 16 * UNITS)
                    degrees(i * 2 + 2, GROUPS - 1, 0, Q)

            act.wait_ge(zeros_used, 1)
            for R in range(GROUPS):
                act.wait_ge(striped_full[R % 2], 16 * (R // 2) + 16)
                degrees(0, R, 0, Q, first=True)
                if R == 6:
                    act.wait_ge(h0_ready, CHUNKS)
                    for g in range(2, 4):
                        strips(act, g, strip_in[:, 0, :, :], CW, SW, group_blocks(0)).then_inc(strip_full[0], 16)
            with act.Fori(0, SUPER - 1) as i:
                superpanel(i)
            superpanel(SUPER - 1, last=True)
            act.wait_ge(sum_ready, 1)
            for b in range(BANKS):
                act.copy(hT[:, b, :], H[b][:, :]).then_inc(hT_ready, 1)
            mid = [TA[0], TA[1], TT, H[0], H[1]]
            for b in range(BANKS):
                act.wait_ge(hc_psum, b + 1)
                act.activation(sq[:, tiles(b), :].rearrange("p (h q) e -> p q h e", h=2),
                               mid[b][:, :].rearrange("p (q h e) -> p q h e", q=Q, h=2),
                               ACT.Square).then_inc(hsq_ready, 1)
            act.wait_ge(hvar_ready, 1)
            act.activation(s2[:, :], s1[:, :], ACT.Sqrt).then_inc(hstd_ready, 1)
            for b in range(BANKS):
                act.wait_ge(c1_ready, b + 1)
                act.activation(sq[:, tiles(b), :], cen[:, tiles(b), :], ACT.Square).then_inc(c1sq_ready, 1)
            act.wait_ge(c1var_ready, 1)
            act.activation(s2[:, :], s1[:, :], ACT.Sqrt).then_inc(c1std_ready, 1)
            act.wait_ge(f_ready, CHUNKS)
            for g in range(1):
                for q in range(4):
                    cp = act.copy(f_cols[BLK * g:BLK * g + BLK, :, :].rearrange("p (a q) e -> p a q e", q=4)[:, :, q, :],
                                  f_sb[BLK * q:BLK * q + BLK, 10 * g:10 * g + 10, :])
            cp.then_inc(fcols_act, 1)

            def group_b(R, u, loads=UNITS, first=False):
                for v in range(UNITS):
                    if v < loads:
                        act.wait_ge(unit_t_full, R * (2 * UNITS) + 2 * (v + 1))
                        for g in range(2, 4):
                            strips(act, g, unit_in[:, v, :, :], v * UW, QUARTER, group_blocks(R + 1))\
                                .then_inc(unit_full[v], 16)
                    if v == 2:
                        act.wait_ge(fT_psum, R + 1)
                        if not first:
                            act.wait_ge(out_psum, R - 1)
                        act.copy(fT[:, u, :, :], TA[0][:, 0:2 * P].rearrange("p (j r) -> p j r", j=2))\
                            .then_inc(fT_ready, 1)
                act.wait_ge(unit_used, R * UNITS + UNITS)
                act.copy(nT[:, u, :], H[u][:, :]).then_inc(nT_ready, 1)

            group_b(0, 0, first=True)
            group_b(1, 1, first=True)
            with act.Fori(1, GROUPS // 2 - 1) as it:
                group_b(it * 2, 0)
                group_b(it * 2 + 1, 1)
            group_b(GROUPS - 2, 0, loads=UNITS - 1)
            group_b(GROUPS - 1, 1, loads=0)

        @block.vector
        def _(dve):
            chain = [0]

            def link(ins):
                chain[0] += 1
                ins.then_inc(dve_chain, 1)
                dve.wait_ge(dve_chain, chain[0])

            def inverse(t):
                link(dve.reciprocal(rs[:, t], s2[:, t]))
                link(dve.tensor_tensor(sn[:, t], rs[:, t], rs[:, t], ALU.mult))
                link(dve.tensor_tensor(sn[:, t], sn[:, t], s1[:, t], ALU.mult))
                link(dve.tensor_scalar(sn[:, t], sn[:, t], -0.5, 1.5, ALU.mult, ALU.add))
                link(dve.tensor_tensor(rs[:, t], rs[:, t], sn[:, t], ALU.mult))

            dve.wait_ge(ident_step, 3)
            for a in (0, HALF):
                link(dve.memset(center[a:a + HALF, a:a + HALF], -1.0 / E))
            for w in (w_user, w_item, w1T):
                dve.memset(w[0:E, E:P], 0.0)
                link(dve.memset(w[E:P, 0:E], 0.0))
            link(dve.tensor_tensor(center[:, :], center[:, :], ident[:, :], ALU.add))

            def constants():
                dve.wait_ge(const_t, 1)
                dve.wait_ge(const_full, 16 * 14)
                link(dve.tensor_copy(w1T[0:E, 0:E], TA[0][0:E, 64:128]))
                link(dve.tensor_copy(w1T[E:P, E:P], TA[0][E:P, 128:192]))
                link(dve.tensor_copy(w2T[0:E, :], TA[0][0:E, 128:192]))
                link(dve.tensor_copy(w2T[E:P, :], TA[0][E:P, 64:128]))
                link(dve.tensor_tensor(parp[:, :], par[:, 0:4:2], par[:, 1:4:2], ALU.mult))
                NU = N_USERS // P
                link(dve.tensor_scalar(scale[:, 0:NU], TA[0][:, 0:NU], parp[:, 0:1], None, ALU.mult))
                dve.tensor_scalar(scale[:, NU:TILES], TA[0][:, NU:TILES], parp[:, 1:2], None, ALU.mult)\
                    .then_inc(consts_ready, 1)

            def normalize(k):
                t = tiles(k)
                dve.wait_ge(x_full[k], 16)
                link(dve.tensor_reduce(s1[:, t], xs[:, t, :], AX, ALU.add))
                link(dve.tensor_scalar(s1[:, t], s1[:, t], 1.0 / E, None, ALU.mult))
                dve.tensor_tensor(cen[:, t, :], xs[:, t, :], both(s1[:, t], CT), ALU.subtract)\
                    .then_inc(cen_ready, 1)
                dve.wait_ge(sq_ready, k + 1)
                link(dve.tensor_reduce(s1[:, t], sq[:, t, :], AX, ALU.add))
                dve.tensor_scalar(s1[:, t], s1[:, t], 1.0 / E, EPS, ALU.mult, ALU.add).then_inc(var_ready, 1)
                dve.wait_ge(std_ready, k + 1)
                inverse(t)
                dve.scalar_tensor_tensor(h0[:, t, :], cen[:, t, :], 0.0, both(rs[:, t], CT), ALU.max,
                                         ALU.mult).then_inc(h0_ready, 1)

            def embed(k):
                t = tiles(k)
                dve.wait_ge(hw_psum, k + 1)
                link(dve.tensor_tensor(e_sb[:, t, :], TA[1][:, :].rearrange("p (t e) -> p t e", t=CT),
                                       both(scale[:, t], CT), ALU.mult))
                dve.tensor_tensor(e_sb[:, t, :], e_sb[:, t, :], h0[:, t, :], ALU.add).then_inc(e_ready, 1)

            for k in range(CHUNKS):
                normalize(k)
                if k == 0:
                    constants()
                else:
                    embed(k - 1)
            embed(CHUNKS - 1)

            def degrees(i2, i1, R):
                dve.wait_ge(turned_full[R], i1 * 16)
                place = degp[:, i2, Q * R:Q * R + Q] if isinstance(i2, int) else \
                    degp[:, bass.ds(i2, 1), Q * R:Q * R + Q].rearrange("p j q -> p (j q)")
                dve.tensor_reduce(place, turned[:, R, :, :], AX, ALU.add).then_inc(deg_turned, Q)

            def superpanel(i, last=False):
                for R in range(GROUPS):
                    dve.wait_ge(strip_full[R % 2], i * (64 * UNITS) + (64 * (R // 2) + 64))
                    if R >= 2:
                        dve.wait_ge(strip_used, i * GROUPS + (R - 1))
                    elif R == 0:
                        dve.wait_ge(shared, i * TILES + TILES)
                    dve.transpose(strip_t[:, R % 2, :, :].rearrange("p c (b k) -> p b c k", k=BLK),
                                  strip_in[:, R % 2, :, :].rearrange("p b (c k) -> p b c k", k=BLK))\
                        .then_inc(strip_t_full, 1)
                    if R and not last:
                        degrees(i * 2 + 2, i + 2, R - 1)
                if not last:
                    degrees(i * 2 + 2, i + 2, GROUPS - 1)

            for R in range(GROUPS):
                degrees(0, 1, R)
            with dve.Fori(0, SUPER - 1) as i:
                superpanel(i)
            superpanel(SUPER - 1, last=True)

            def transpose_unit(src, k):
                for half in range(2):
                    b = slice(half * (GW // BLK // 2), (half + 1) * (GW // BLK // 2))
                    r = slice(half * (GW // 2), (half + 1) * (GW // 2))
                    dve.transpose(unit_t[:, k, :, r].rearrange("p c (b k) -> p b c k", k=BLK),
                                  src[:, b, :].rearrange("p b (c k) -> p b c k", k=BLK))\
                        .then_inc(unit_t_full, 1)

            dve.wait_ge(deg_turned, SUPER * TILES)
            dve.wait_ge(deg_striped, SUPER * TILES)
            link(dve.tensor_reduce(rdeg[:, :], degp[:, :, :].rearrange("p j c -> p c j"), AX, ALU.add))
            link(dve.tensor_scalar(rdeg[:, :], rdeg[:, :], 1.0, None, ALU.add))
            link(dve.reciprocal(rdeg[:, :], rdeg[:, :]))
            dve.wait_ge(sum_ready, 1)
            for m in range(2):
                dve.wait_ge(unit_full[m], 64)
                transpose_unit(unit_in[:, m, :, :], m)

            mid = [TA[0], TA[1], TT, H[0], H[1]]
            for b in range(BANKS):
                dve.wait_ge(hsq_ready, b + 1)
                link(dve.tensor_reduce(s1[:, tiles(b)], sq[:, tiles(b), :], AX, ALU.add))
            dve.tensor_scalar(s1[:, :], s1[:, :], 1.0 / E, EPS, ALU.mult, ALU.add).then_inc(hvar_ready, 1)
            dve.wait_ge(hstd_ready, 1)
            inverse(slice(0, TILES))
            dve.wait_ge(res_ready, CHUNKS)
            for b in range(BANKS):
                t = tiles(b)
                for h in range(2):
                    th = slice(CT * b + Q * h, CT * b + Q * h + Q)
                    link(dve.tensor_tensor(cen[:, th, :], mid[b][:, :].rearrange("p (q h e) -> p h q e", q=Q, h=2)[:, h],
                                           both(rs[:, th], Q), ALU.mult))
                link(dve.tensor_tensor(cen[:, t, :], cen[:, t, :], rows(gam[:, :], CT), ALU.mult))
                link(dve.tensor_tensor(xs[:, t, :], cen[:, t, :], res[:, t, :], ALU.add))
                link(dve.tensor_reduce(s1[:, t], xs[:, t, :], AX, ALU.add))
            link(dve.tensor_scalar(s1[:, :], s1[:, :], 1.0 / E, None, ALU.mult))
            for b in range(BANKS):
                t = tiles(b)
                dve.tensor_tensor(cen[:, t, :], xs[:, t, :], both(s1[:, t], CT), ALU.subtract).then_inc(c1_ready, 1)
            for b in range(BANKS):
                t = tiles(b)
                dve.wait_ge(c1sq_ready, b + 1)
                link(dve.tensor_reduce(s1[:, t], sq[:, t, :], AX, ALU.add))
            dve.tensor_scalar(s1[:, :], s1[:, :], 1.0 / E, EPS, ALU.mult, ALU.add).then_inc(c1var_ready, 1)
            dve.wait_ge(c1std_ready, 1)
            inverse(slice(0, TILES))
            for b in range(BANKS):
                t = tiles(b)
                dve.scalar_tensor_tensor(f_sb[:, t, :], cen[:, t, :], 0.0, both(rs[:, t], CT), ALU.max,
                                         ALU.mult).then_inc(f_ready, 1)
            dve.wait_ge(f_ready, CHUNKS)
            for g in range(1, 4):
                for q in range(4):
                    cp = dve.tensor_copy(f_cols[BLK * g:BLK * g + BLK, :, :].rearrange("p (a q) e -> p a q e", q=4)[:, :, q, :],
                                         f_sb[BLK * q:BLK * q + BLK, 10 * g:10 * g + 10, :])
            cp.then_inc(fcols_dve, 1)

            def group_out(R1, R_half, u, first=False):
                cols = TA[1][:, :].rearrange("p (w q e) -> p w q e", q=Q, w=2)
                dve.wait_ge(out_psum, R1)
                if not (isinstance(R1, int) and R1 == 1):
                    dve.wait_ge(obuf_ready, R1 - 1)
                t = slice(Q * R1 - Q, Q * R1) if isinstance(R1, int) else bass.ds(R1 * Q - Q, Q)
                dve.tensor_tensor(o1[:, :, :], cols[:, 1, :, :], both(rdeg[:, t], Q), ALU.mult)\
                    .then_inc(o1_ready, 1)
                dve.tensor_tensor(o2[:, :, :], cols[:, 0, :, :], xs[:, t, :], ALU.add).then_inc(o2_ready, 1)
                dve.wait_ge(o1_ready, R1)
                dve.wait_ge(o2_ready, R1)
                if not first:
                    dve.wait_ge(stored[u], R_half * 16)
                dve.tensor_tensor(obuf[:, u, :, :], o1[:, :, :], o2[:, :, :], ALU.add).then_inc(obuf_ready, 1)

            def units_ahead(R, u, loads, n=UNITS):
                for w in range(2, 2 + n):
                    if n < UNITS and w == UNITS - 1:
                        dve.wait_ge(last_full, 64)
                    else:
                        dve.wait_ge(unit_full[w % UNITS], loads + w // UNITS * 64)
                    dve.wait_ge(unit_used, R * UNITS + (w - 1))
                    src = last_in if n < UNITS and w == UNITS - 1 else unit_in[:, w % UNITS, :, :]
                    transpose_unit(src, (UNITS * u + w) % 2)

            units_ahead(0, 0, 64)
            units_ahead(1, 1, 128)
            group_out(1, 0, 0, first=True)
            units_ahead(2, 0, 192)
            group_out(2, 0, 1, first=True)
            with dve.Fori(1, GROUPS // 2 - 1) as it:
                units_ahead(it * 2 + 1, 1, it * 128 + 128)
                group_out(it * 2 + 1, it, 0)
                units_ahead(it * 2 + 2, 0, it * 128 + 192)
                group_out(it * 2 + 2, it, 1)
            units_ahead(GROUPS - 1, 1, 64 * GROUPS, n=UNITS - 2)
            group_out(GROUPS - 1, GROUPS // 2 - 1, 0)
            group_out(GROUPS, GROUPS // 2 - 1, 1)


_INS = ['x', 'adj', 'L0_gnn_W_u', 'L0_gnn_diag_u', 'L0_gnn_par_u', 'L0_gnn_W_i', 'L0_gnn_diag_i',
        'L0_gnn_par_i', 'L0_gnn_ln_gamma', 'L0_gnn_ln_beta', 'L1_gnn_W']
_OUTS = [((5120, 64), 'float32')]


def kernel(**inputs):
    import numpy as _np
    import concourse.bacc as _bacc
    from concourse import mybir as _mybir
    from concourse.bass_utils import run_bass_kernel_spmd as _run

    nc = _bacc.Bacc("TRN2", target_bir_lowering=False, num_devices=1)
    arrays, args = {}, []
    for name in _INS:
        a = _np.ascontiguousarray(inputs[name])
        arrays[f"in_{name}_dram"] = a
        args.append(nc.dram_tensor(f"in_{name}_dram", a.shape, _mybir.dt.from_np(a.dtype), kind="ExternalInput").ap())
    for i, (shape, dtype) in enumerate(_OUTS):
        dt = _mybir.dt.from_np(_np.dtype(dtype))
        args.append(nc.dram_tensor(f"out_{i}_dram", shape, dt, kind="ExternalOutput").ap())
    gnn_kernel(nc, *args)
    r = _run(nc, [arrays], core_ids=[0])
    got = tuple(r.results[0][f"out_{i}_dram"] for i in range(len(_OUTS)))
    return got[0]
```

```python
from contextlib import ExitStack

import concourse.bass as bass
from concourse import mybir

F32 = mybir.dt.float32
ALU = mybir.AluOpType
ACT = mybir.ActivationFunctionType
AX = mybir.AxisListType.X

P = 128
HALF = 64
BLK = 32
EPS = 1e-5


def gnn_kernel(nc, x, adj, w_u, diag_u, par_u, w_i, diag_i, par_i, gamma, beta, w_l1, out):
    N, E = x.shape
    N_USERS = diag_u.shape[0]
    assert E == HALF and w_l1.shape[0] == E
    TILES = N // P
    Q = 4
    GW = Q * P
    GROUPS = N // GW
    CW = 512
    CC = CW // P
    SW = CW // 4
    SUPER = N // (2 * CW)
    TURNS = GROUPS * CC + 1
    BANKS = GROUPS // 2
    CHUNKS = TILES // 8
    CT = 8
    QUARTER = N // 4
    UW = 256
    UNITS = QUARTER // UW
    UC = UW // BLK
    POOL_CHUNKS = [0, 2, 3]
    C1_ORDER = [1, 0, 2, 4, 3]
    assert CC == Q and UNITS * 2 == GROUPS and CW == 2 * UW and N_USERS % (CT * P) == 0

    with ExitStack() as ctx:
        def sb(name, shape):
            return ctx.enter_context(nc.sbuf_tensor(name, shape, F32))

        def bank(name):
            return ctx.enter_context(nc.psum_tensor(name, [P, 512], F32))

        def sem(name):
            return ctx.enter_context(nc.semaphore(name))

        turned = sb("turned", [P, GROUPS, Q, CW])
        striped = sb("striped", [P, 2, Q, CW])
        unit_in = turned[:, :, :, :].rearrange("p (s a) q c -> p s (a q c)", s=UNITS).rearrange(
            "p s (b c) -> p s b c", c=UW)
        last_in = striped[:, :, :, :].rearrange("p a q c -> p (a q c)").rearrange(
            "p (b c) -> p b c", c=UW)
        unit_t = sb("unit_t", [P, 2, UC, GW])
        turned_t = unit_t[:, 0, :, :].rearrange("p (s c) r -> p s c r", s=2)
        strip_t = unit_t[:, 1, :, :].rearrange("p (s c) r -> p s c r", s=2)
        work = sb("work", [P, 3 * TILES * E])
        cen, sq, h0 = (work[:, i * TILES * E:(i + 1) * TILES * E].rearrange("p (t e) -> p t e", e=E)
                       for i in range(3))
        f_cols = h0
        strip_in = work[:, 0:2 * GW // BLK * SW].rearrange("p (s b c) -> p s b c", s=2, c=SW)
        first_place = [striped[:, 0], striped[:, 1],
                       strip_in[:, 1].rearrange("p b c -> p (b c)").rearrange("p (q c) -> p q c", q=Q)]
        FIRST = [(R + 1) % 3 for R in range(GROUPS)]
        xs = sb("xs", [P, TILES, E])
        e_sb = sb("e_sb", [P, TILES, E])
        f_sb = e_sb
        spare = sb("spare", [P, 2 * TILES * E])
        hT = spare[:, 0:BANKS * GW].rearrange("p (b r) -> p b r", b=BANKS)
        res = spare[:, TILES * E:2 * TILES * E].rearrange("p (t e) -> p t e", e=E)
        third_t = spare[:, 0:UC * GW].rearrange("p (c r) -> p c r", c=UC)
        last_turned = h0.rearrange("p t e -> p (t e)")[:, 0:CC * GW].rearrange("p (c r) -> p c r", c=CC)
        last_strips = [hT[:, 0:CC, :],
                       e_sb[:, :, :].rearrange("p t e -> p (t e)")[:, 0:CC * GW].rearrange("p (c r) -> p c r", c=CC)]
        junk = hT[:, 1:5, :]
        degp = sb("degp", [P, 2 * SUPER, TILES])
        rdeg = sb("rdeg", [P, TILES])
        h0T = unit_t[:, 0, 0, :].rearrange("p (j r) -> p j r", j=Q)
        w_user = unit_t[:, 0, 1, 0:P]
        w_item = unit_t[:, 0, 1, P:2 * P]
        wl = unit_t[0:E, 0, 2, 0:2 * E]
        wl_sw = unit_t[0:E, 0, 2, 2 * E:4 * E]
        diag = unit_t[0:TILES, 0, 3, 0:P]
        gam = unit_t[:, 0, 3, P:P + 1]
        gam_center = unit_t[:, 0, 4, 0:P + 2]
        zero_w = unit_t[:, 0, 5, 0:E]
        tT = sb("tT", [P, CW])
        t_sb = sb("t_sb", [P, CC, 2, E])
        ident = sb("ident", [P, P])
        center = sb("center", [P, P])
        turn_center = sb("turn_center", [P, P + 2])
        w1T = sb("w1T", [P, P])
        w2T = sb("w2T", [P, E])
        par = sb("par", [P, 4])
        parp = sb("parp", [P, 2])
        scale = sb("scale", [P, TILES])
        res_mean = sb("res_mean", [P, TILES])
        x1_mean = sb("x1_mean", [P, TILES])
        bet = sb("bet", [P, E])
        s1 = sb("s1", [P, TILES])
        s2 = sb("s2", [P, TILES])
        rs = sb("rs", [P, TILES])
        sn = sb("sn", [P, TILES])
        after = 0

        def place(n):
            nonlocal after
            after += n
            assert after <= 2 * TILES * E
            return work[:, after - n:after]

        stage = place(2 * Q * E).rearrange("p (u q e) -> p u q e", u=2, q=Q)
        fT = place(2 * 2 * P).rearrange("p (u j r) -> p u j r", u=2, j=2)
        nT = place(2 * GW).rearrange("p (u r) -> p u r", u=2)
        o1 = place(Q * E).rearrange("p (q e) -> p q e", q=Q)
        o2 = place(Q * E).rearrange("p (q e) -> p q e", q=Q)
        obuf = place(2 * Q * E).rearrange("p (u q e) -> p u q e", u=2, q=Q)

        H = [bank(f"H{b}") for b in range(BANKS)]
        TT = bank("TT")
        TA = [bank("TA0"), bank("TA1")]
        mid = [TA[0], TA[1], TT, H[0], H[1]]
        midg = [H[2], H[3], H[4], TA[0], TA[1]]

        x_full = [sem(f"x_full{c}") for c in range(CHUNKS)]
        const_full = sem("const_full")
        wi_full = sem("wi_full")
        late_full = sem("late_full")
        turned_full = [sem(f"turned_full{R}") for R in range(GROUPS)]
        first_full = [sem(f"first_full{k}") for k in range(3)]
        striped_full = [sem(f"striped_full{k}") for k in range(2)]
        strip_full = [sem(f"strip_full{k}") for k in range(2)]
        last_full = sem("last_full")
        half_full = [sem("half_full0"), sem("half_full1")]
        unit_full = [sem(f"unit_full{s}") for s in range(UNITS)]
        ident_step = sem("ident_step")
        zeros_ready = sem("zeros_ready")
        zeros_used = sem("zeros_used")
        consts_ready = sem("consts_ready")
        dve_chain = sem("dve_chain")
        pool_chain = sem("pool_chain")
        const_t = sem("const_t")
        late_t = sem("late_t")
        gam_ready = sem("gam_ready")
        late_ready = sem("late_ready")
        res_mid = sem("res_mid")
        mean_psum = sem("mean_psum")
        gc_psum = sem("gc_psum")
        cr_ready = sem("cr_ready")
        x1_mean_ready = sem("x1_mean_ready")
        cen_ready = sem("cen_ready")
        sq_ready = sem("sq_ready")
        var_ready = sem("var_ready")
        std_ready = sem("std_ready")
        h0_ready = sem("h0_ready")
        h0T_psum = sem("h0T_psum")
        h0T_ready = sem("h0T_ready")
        hw_psum = sem("hw_psum")
        e_ready = sem("e_ready")
        res_ready = sem("res_ready")
        blocks_t = sem("blocks_t")
        t_psum = sem("t_psum")
        turn_full = sem("turn_full")
        turned_used = sem("turned_used")
        strip_t_full = sem("strip_t_full")
        strip_used = sem("strip_used")
        shared = sem("shared")
        tT_ready = sem("tT_ready")
        deg_turned = sem("deg_turned")
        deg_striped = sem("deg_striped")
        sum_ready = sem("sum_ready")
        hT_ready = sem("hT_ready")
        hc_psum = sem("hc_psum")
        hsq_ready = sem("hsq_ready")
        hstd_ready = sem("hstd_ready")
        hvar_ready = sem("hvar_ready")
        c1_ready = sem("c1_ready")
        c1_pool = sem("c1_pool")
        x1_ready = sem("x1_ready")
        c1sq_ready = sem("c1sq_ready")
        c1var_ready = sem("c1var_ready")
        c1std_ready = sem("c1std_ready")
        f_ready = sem("f_ready")
        fcols_dve = sem("fcols_dve")
        fcols_act = sem("fcols_act")
        unit_t_full = sem("unit_t_full")
        unit_used = sem("unit_used")
        nT_ready = sem("nT_ready")
        stage_ready = sem("stage_ready")
        fT_psum = sem("fT_psum")
        fT_ready = sem("fT_ready")
        out_psum = sem("out_psum")
        o1_ready = sem("o1_ready")
        o2_ready = sem("o2_ready")
        obuf_ready = sem("obuf_ready")
        stored = [sem("stored0"), sem("stored1")]

        x_v = x.rearrange("(c p) e -> p c e", p=P)
        a_panel = adj.rearrange("(r q p) c -> r p q c", q=Q, p=P)
        a_strip = adj.rearrange("(b k) c -> k b c", k=BLK)
        out_v = out.rearrange("(c p) e -> p c e", p=P)

        def both(ap, n):
            return ap.unsqueeze(2).to_broadcast([P, n, E])

        def rows(ap, n):
            return ap.unsqueeze(1).to_broadcast([P, n, E])

        def tiles(k):
            return slice(CT * k, CT * k + CT)

        def strips(eng, g, dst, col, quarter, blocks):
            w = dst.shape[2]
            cols = slice(col + g * quarter, col + g * quarter + w) if isinstance(col, int) \
                else bass.ds(col + g * quarter, w)
            return eng.dma_start(dst[BLK * g:BLK * g + BLK, :, :], a_strip[:, blocks, cols])

        def group_blocks(R):
            n = GW // BLK
            return slice(n * R, n * R + n) if isinstance(R, int) else bass.ds(R * n, n)

        def at(R, k):
            return isinstance(R, int) and R == k

        F_SPANS = [(0, 2 * UC // 4), (2 * UC // 4, TILES // 4)]

        def f_columns(copy, g, q, a, b):
            return copy(f_cols[BLK * g:BLK * g + BLK, :, :].rearrange("p (a q) e -> p a q e", q=4)[:, a:b, q, :],
                        f_sb[BLK * q:BLK * q + BLK, TILES // 4 * g + a:TILES // 4 * g + b, :])

        def half_in(half):
            return unit_in[:, UNITS - 1, :, half * UW // 2:(half + 1) * UW // 2]

        def unit_place(m):
            return unit_t[:, m, :, :] if m < 2 else third_t if m == 2 else unit_t[:, (m - 1) % 2, :, :]

        def turned_place(R, last):
            return last_turned if last and R == GROUPS - 1 else turned_t[:, R % 2]

        def strip_place(R, last):
            return last_strips[R - GROUPS + 2] if last and R >= GROUPS - 2 else strip_t[:, R % 2]

        def turn(R, c):
            return R * CC + c + (1 if R else 0)

        block = ctx.enter_context(nc.Block())

        @block.sync
        def _(sp):
            for k in range(CHUNKS):
                sp.dma_start(xs[:, tiles(k), :], x_v[:, tiles(k), :]).then_inc(x_full[k], 16)

            def load_turned(R, col):
                sp.dma_start(turned[:, R, :, :], a_panel[R][:, :, col]).then_inc(turned_full[R], 16)

            def load_striped(R, col):
                sp.dma_start(striped[:, R % 2, :, :], a_panel[R][:, :, col]).then_inc(striped_full[R % 2], 16)

            turned_by = [0, 1, 4, 4, 5, 6, 7, 8, 9, 10, 10]
            for R in range(GROUPS):
                for r in range(turned_by[R], turned_by[R + 1]):
                    load_turned(r, slice(0, CW))
                before = [r for r in range(R) if FIRST[r] == FIRST[R]]
                if before:
                    sp.wait_ge(shared, Q * (before[-1] + 1))
                    sp.wait_ge(deg_striped, Q * (before[-1] + 1))
                elif FIRST[R] == 2:
                    sp.wait_ge(h0_ready, CHUNKS)
                sp.dma_start(first_place[FIRST[R]], a_panel[R][:, :, CW:2 * CW]).then_inc(first_full[FIRST[R]], 16)
            for g in range(2):
                strips(sp, g, strip_in[:, 0, :, :], CW, SW, group_blocks(0)).then_inc(strip_full[0], 16)

            with sp.Fori(0, SUPER - 1) as i:
                for R in range(GROUPS):
                    before = sp.snap(i * TILES + Q * (GROUPS + R - 1))
                    col = sp.snap(i * (2 * CW) + 3 * CW)
                    sp.wait_ge(shared, before)
                    sp.wait_ge(deg_striped, before)
                    load_striped(R, bass.ds(col, CW))
                    read = sp.snap(i * TILES + Q * (R + 1))
                    col = sp.snap(i * (2 * CW) + 2 * CW)
                    sp.wait_ge(blocks_t, read)
                    sp.wait_ge(deg_turned, read)
                    load_turned(R, bass.ds(col, CW))
                    if R:
                        free = sp.snap(i * GROUPS + R)
                    cols = [sp.snap(i * (2 * CW) + ((CW if R < GROUPS - 1 else 3 * CW) + g * SW)) for g in range(2)]
                    if R:
                        sp.wait_ge(strip_t_full, free)
                    for g in range(2):
                        strips(sp, g, strip_in[:, (R + 1) % 2, :, :], cols[g], 0, group_blocks((R + 1) % GROUPS))\
                            .then_inc(strip_full[(R + 1) % 2], 16)
            sp.wait_ge(shared, SUPER * TILES)
            sp.wait_ge(deg_striped, SUPER * TILES)
            sp.wait_ge(deg_turned, SUPER * TILES)
            for R in range(GROUPS):
                if R < GROUPS - 1:
                    sp.wait_ge(strip_t_full, (SUPER - 1) * GROUPS + R)
                    for g in range(2):
                        strips(sp, g, strip_in[:, (R + 1) % 2, :, :], (2 * SUPER - 1) * CW, SW,
                               group_blocks(R + 1)).then_inc(strip_full[(R + 1) % 2], 16)
                if R == 0:
                    for g in range(2):
                        strips(sp, g, last_in, 0, QUARTER, group_blocks(GROUPS - 1))\
                            .then_inc(last_full, 16)
                if R % 2:
                    m = R // 2
                    sp.wait_ge(blocks_t, (SUPER - 1) * TILES + Q * (R + 1))
                    for g in range(2):
                        strips(sp, g, unit_in[:, m, :, :], m * UW, QUARTER, group_blocks(0))\
                            .then_inc(unit_full[m], 16)

            def load_units(R, units=range(UNITS)):
                for v in units:
                    sp.wait_ge(unit_t_full, R * (2 * UNITS) + (2 * (v + 1) - 2 * UNITS))
                    for g in range(2):
                        strips(sp, g, unit_in[:, v, :, :], v * UW, QUARTER, group_blocks(R))\
                            .then_inc(unit_full[v], 16)

            sp.wait_ge(unit_t_full, 3)
            with sp.Fori(1, GROUPS - 1) as R:
                load_units(R)
            load_units(GROUPS - 1, range(1, UNITS - 1))
            sp.wait_ge(unit_t_full, 2 * UNITS * (GROUPS - 1))
            for half in range(2):
                for g in range(2):
                    strips(sp, g, half_in(half), (UNITS - 1) * UW + half * UW // 2, QUARTER, group_blocks(GROUPS - 1))\
                        .then_inc(half_full[half], 16)
            for s in range(2):
                sp.wait_ge(stored[s], 16 * (GROUPS // 2))

        @block.gpsimd
        def _(pool):
            pool.memset(ident[:, :], 0.0).then_inc(ident_step, 1)
            pool.memset(zero_w[:, :], 0.0).then_inc(zeros_ready, 1)
            pool.memset(hT[:, 0, :], 0.0).then_inc(zeros_ready, 1)
            pool.memset(center[:, :], 0.0).then_inc(ident_step, 1)
            pool.wait_ge(ident_step, 2)
            pool.affine_select(out=ident[:, :], in_=ident[:, :], compare_op=ALU.not_equal, fill=1.0,
                               base=0, pattern=[[-1, P]], channel_multiplier=1).then_inc(ident_step, 1)
            pool.wait_ge(late_full, 16 * 7)
            for k in range(CHUNKS):
                pool.wait_ge(h0_ready, k + 1)
                pool.tensor_tensor(res[:, tiles(k), :], xs[:, tiles(k), :], h0[:, tiles(k), :], ALU.add)\
                    .then_inc(pool_chain, 1)
                pool.wait_ge(pool_chain, k + 1)
                pool.tensor_tensor(res[:, tiles(k), :], res[:, tiles(k), :], rows(bet[:, :], CT), ALU.add)\
                    .then_inc(res_ready, 1)
            for b in POOL_CHUNKS:
                pool.wait_ge(cr_ready, 2 * b + 2)
                pool.tensor_tensor(cen[:, tiles(b), :], cen[:, tiles(b), :], res[:, tiles(b), :], ALU.add)\
                    .then_inc(c1_pool, 1)
            pool.wait_ge(x1_mean_ready, 1)
            pool.wait_ge(c1_pool, len(POOL_CHUNKS))
            pool.wait_ge(c1_ready, BANKS - len(POOL_CHUNKS))
            for b in range(BANKS):
                pool.tensor_tensor(xs[:, tiles(b), :], cen[:, tiles(b), :], both(x1_mean[:, tiles(b)], CT), ALU.add)\
                    .then_inc(x1_ready, 1)
            pool.wait_ge(x1_ready, CHUNKS)
            pool.wait_ge(f_ready, CHUNKS)
            for u in range(2):
                pool.tensor_copy(stage[:, u, :, :], f_sb[:, Q * u:Q * u + Q, :]).then_inc(stage_ready, 1)

            def store(R, u):
                pool.wait_ge(obuf_ready, R + 1)
                t = slice(Q * R, Q * R + Q) if isinstance(R, int) else bass.ds(R * Q, Q)
                pool.dma_start(out_v[:, t, :], obuf[:, u, :, :]).then_inc(stored[u], 16)

            with pool.Fori(0, GROUPS // 2 - 1) as it:
                for u in range(2):
                    store(it * 2 + u, u)
                    pool.wait_ge(fT_psum, it * 2 + (u + 1))
                    pool.tensor_copy(stage[:, u, :, :], f_sb[:, bass.ds(it * (2 * Q) + (2 + u) * Q, Q), :])\
                        .then_inc(stage_ready, 1)
            for u in range(2):
                store(GROUPS - 2 + u, u)

        @block.tensor
        def _(pe):
            pe.wait_ge(ident_step, 3)
            pe.wait_ge(zeros_ready, 2)
            for R in range(GROUPS):
                a = HALF * (R % 2)
                mm = pe.matmul(H[R // 2][a:a + HALF, :], zero_w[:, :], hT[:, 0, :], start=True, stop=False,
                               skip_group_check=True)
            mm.then_inc(zeros_used, 1)
            pe.wait_ge(const_full, 16 * 6)
            pe.transpose(TA[0][:, 0:TILES], diag[:, :], ident[0:TILES, 0:TILES]).then_inc(const_t, 1)
            pe.wait_ge(consts_ready, 1)

            def turn_h0(k):
                pe.wait_ge(h0_ready, k + 1)
                if k:
                    pe.wait_ge(h0T_ready, k)
                for j in range(Q):
                    pair = h0[:, CT * k + 2 * j:CT * k + 2 * j + 2, :].rearrange("p t e -> p (t e)")
                    mm = pe.transpose(TA[0][:, j * P:(j + 1) * P], pair, ident[:, :])
                mm.then_inc(h0T_psum, 1)

            def times_w(k):
                pe.wait_ge(h0T_ready, k + 1)
                if k:
                    pe.wait_ge(e_ready, k)
                w = w_user if CT * k * P < N_USERS else w_item
                if w is w_item:
                    pe.wait_ge(wi_full, 16 * 2)
                for j in range(Q):
                    mm = pe.matmul(TA[1][:, j * P:(j + 1) * P], h0T[:, j, :], w[:, :], start=True, stop=True)
                mm.then_inc(hw_psum, 1)

            def share_turned(R, q):
                return pe.matmul(TT[0:HALF, :], e_sb[:, Q * R + q, :], turned[:, R, q, :],
                                 start=(R == 0 and q == 0), stop=(R == GROUPS - 1 and q == Q - 1),
                                 skip_group_check=True)

            def share_striped(R, q, place=None):
                place = striped[:, R % 2] if place is None else place
                return pe.matmul(TT[HALF:P, :], e_sb[:, Q * R + q, :], place[:, q, :],
                                 start=(R == 0 and q == 0), stop=(R == GROUPS - 1 and q == Q - 1),
                                 skip_group_check=True)

            def wait_loads(i1, R):
                pe.wait_ge(turned_full[R], i1 * 16)
                pe.wait_ge(striped_full[R % 2], (i1 - 2) * (16 * UNITS) + (16 * (R // 2) + 16))

            def share(i1, R):
                wait_loads(i1, R)
                for q in range(Q):
                    share_turned(R, q)
                    mm = share_striped(R, q)
                mm.then_inc(shared, Q)

            def share_first(R):
                pe.wait_ge(turned_full[R], 16)
                pe.wait_ge(first_full[FIRST[R]], 16 * (FIRST[:R].count(FIRST[R]) + 1))
                for q in range(Q):
                    share_turned(R, q)
                    mm = share_striped(R, q, first_place[FIRST[R]])
                mm.then_inc(shared, Q)

            def turn_blocks(i, R, c):
                k = turn(R, c)
                if k >= 2:
                    pe.wait_ge(turn_full, i * TURNS + (k - 1))
                for q in range(Q):
                    mm = pe.transpose(TA[k % 2][:, q * P:(q + 1) * P],
                                      turned[:, R, q, c * P:(c + 1) * P], ident[:, :])
                mm.then_inc(blocks_t, 1)

            def add_turned(R, c, last):
                a = HALF * (R % 2)
                mm = pe.matmul(H[R // 2][a:a + HALF, :], t_sb[:, c, 0, :], turned_place(R, last)[:, c, :],
                               start=False, stop=False, skip_group_check=True)
                if c == CC - 1:
                    mm.then_inc(turned_used, 1)

            def add_strip(R, c, last):
                a = HALF * (R % 2)
                mm = pe.matmul(H[R // 2][a:a + HALF, :], t_sb[:, c, 1, :], strip_place(R, last)[:, c, :],
                               start=False, stop=last and c == CC - 1, skip_group_check=True)
                if c == CC - 1:
                    mm.then_inc(sum_ready if last and R == GROUPS - 1 else strip_used, 1)

            def superpanel(i, last=False):
                for R in range(GROUPS):
                    if R == 0:
                        turn_blocks(i, R, 2)
                        turn_blocks(i, R, 3)
                        pe.wait_ge(tT_ready, i * 2 + 2)
                        pe.wait_ge(turn_full, i * TURNS + 3)
                        for c in range(CC):
                            mm = pe.transpose(TA[0][:, c * P:(c + 1) * P], tT[:, c * P:(c + 1) * P],
                                              ident[:, :])
                        mm.then_inc(t_psum, 1)
                        continue
                    turn_blocks(i, R, 0)
                    turn_blocks(i, R, 1)
                    pe.wait_ge(turn_full, i * TURNS + (turn(R - 1, CC - 1) + 1))
                    if R > 1:
                        pe.wait_ge(strip_t_full, i * GROUPS + (R - 1))
                    for c in range(CC):
                        add_turned(R - 1, c, last)
                        if R > 1:
                            add_strip(R - 2, c, last)
                    turn_blocks(i, R, 2)
                    turn_blocks(i, R, 3)
                    if not last:
                        share(i + 2, R - 1)
                pe.wait_ge(turn_full, i * TURNS + TURNS)
                pe.wait_ge(strip_t_full, i * GROUPS + (GROUPS - 1))
                for c in range(CC):
                    add_turned(GROUPS - 1, c, last)
                    add_strip(GROUPS - 2, c, last)
                pe.wait_ge(strip_t_full, i * GROUPS + GROUPS)
                if last:
                    for c in range(CC):
                        add_strip(GROUPS - 1, c, last)
                else:
                    wait_loads(i + 2, GROUPS - 1)
                    for c in range(CC):
                        add_strip(GROUPS - 1, c, last)
                        share_turned(GROUPS - 1, c)
                    turn_blocks(i + 1, 0, 0)
                    turn_blocks(i + 1, 0, 1)
                    for q in range(Q):
                        mm = share_striped(GROUPS - 1, q)
                    mm.then_inc(shared, Q)

            turn_h0(0)
            times_w(0)
            for k in range(CHUNKS):
                if k + 1 < CHUNKS:
                    turn_h0(k + 1)
                pe.wait_ge(e_ready, k + 1)
                if k == CHUNKS - 1:
                    pe.wait_ge(late_full, 16 * 7)
                    pe.transpose(TA[0][:, 0:64], wl[:, :], ident[0:E, 0:E])
                    pe.transpose(TA[0][:, 64:128], wl_sw[:, :], ident[0:E, 0:E])
                    pe.wait_ge(gam_ready, 1)
                    pe.matmul(TA[1][:, 0:P + 2], center[:, :], gam_center[:, :], start=True, stop=True)\
                        .then_inc(late_t, 1)
                share_first(2 * k)
                if k + 1 < CHUNKS:
                    times_w(k + 1)
                share_first(2 * k + 1)
            pe.wait_ge(late_ready, 1)
            turn_blocks(0, 0, 0)
            turn_blocks(0, 0, 1)
            with pe.Fori(0, SUPER - 1) as i:
                superpanel(i)
            superpanel(SUPER - 1, last=True)

            for b in range(BANKS):
                pe.wait_ge(hT_ready, b + 1)
                for q in range(Q):
                    mm = pe.matmul(mid[b][:, q * P:(q + 1) * P], hT[:, b, q * P:(q + 1) * P],
                                   center[:, :], start=True, stop=True)
                mm.then_inc(hc_psum, 1)
            for b in range(BANKS):
                if b < 3:
                    pe.wait_ge(hT_ready, BANKS)
                else:
                    pe.wait_ge(hsq_ready, b - 2)
                for q in range(Q):
                    mm = pe.matmul(midg[b][:, q * P:(q + 1) * P], hT[:, b, q * P:(q + 1) * P],
                                   turn_center[:, 0:P], start=True, stop=True)
                mm.then_inc(gc_psum, 1)
            pe.wait_ge(hsq_ready, 3)
            for b in range(BANKS):
                for q in range(Q):
                    mm = pe.matmul(TT[:, (b * Q + q) * 2:(b * Q + q) * 2 + 2], hT[:, b, q * P:(q + 1) * P],
                                   turn_center[:, P:P + 2], start=True, stop=True)
            mm.then_inc(mean_psum, 1)

            def group_out_t(R1, u):
                pe.wait_ge(stage_ready, R1)
                if not at(R1, 1):
                    pe.wait_ge(fT_ready, R1 - 1)
                for j in range(2):
                    mm = pe.transpose(TA[0][:, j * P:(j + 1) * P],
                                      stage[:, u, 2 * j:2 * j + 2, :].rearrange("p t e -> p (t e)"),
                                      ident[:, :])
                mm.then_inc(fT_psum, 1)

            def group_out(R1, u):
                pe.wait_ge(fT_ready, R1)
                pe.wait_ge(nT_ready, R1)
                if not at(R1, 1):
                    pe.wait_ge(o2_ready, R1 - 1)
                for j in range(2):
                    pe.matmul(TA[1][:, j * P:(j + 1) * P], fT[:, u, j, :], w1T[:, :], start=True, stop=True)
                for q in range(Q):
                    mm = pe.matmul(TA[1][:, (Q + q) * E:(Q + q + 1) * E], nT[:, u, q * P:(q + 1) * P],
                                   w2T[:, :], start=True, stop=True)
                mm.then_inc(out_psum, 1)

            def group_b(R, u, first=False):
                for v in range(UNITS):
                    m = R * UNITS + v
                    if first and R == 0 and v == 2:
                        pe.wait_ge(fcols_dve, 2)
                        pe.wait_ge(fcols_act, 2)
                    place = UNITS * u + v + (0 if at(R, 0) or at(R, 1) else 2 * UNITS)
                    if v == 0 and not first:
                        pe.wait_ge(nT_ready, R - 1)
                    for c in range(UC):
                        if c % (UC // 2) == 0:
                            pe.wait_ge(unit_t_full, m * 2 + (1 + c // (UC // 2)))
                        a = HALF * (c % 2)
                        mm = pe.matmul(H[u][a:a + HALF, :], f_cols[:, UC * v + c, :],
                                       unit_place(place)[:, c, :], start=(v == 0 and c < 2),
                                       stop=(v == UNITS - 1 and c >= UC - 2), skip_group_check=True)
                    mm.then_inc(unit_used, 1)
                    if v == 1:
                        group_out_t(R + 1, u)
                    if v == 3 and not at(R, 0):
                        group_out(R, 1 - u)

            pe.wait_ge(unit_t_full, 3)
            pe.wait_ge(fcols_dve, 1)
            pe.wait_ge(fcols_act, 1)
            group_b(0, 0, first=True)
            group_b(1, 1, first=True)
            with pe.Fori(1, GROUPS // 2) as it:
                group_b(it * 2, 0)
                group_b(it * 2 + 1, 1)
            group_out(GROUPS, 1)

        @block.scalar
        def _(act):
            for dst, src in [(diag[0:N_USERS // P, :], diag_u.rearrange("(c p) -> c p", p=P)),
                             (diag[N_USERS // P:TILES, :], diag_i.rearrange("(c p) -> c p", p=P)),
                             (par[:, 0:2], par_u.partition_broadcast(P)), (par[:, 2:4], par_i.partition_broadcast(P)),
                             (w_user[0:E, 0:E], w_u), (w_user[E:P, E:P], w_u)]:
                act.dma_start(dst, src).then_inc(const_full, 16)
            for a in (0, E):
                act.dma_start(w_item[a:a + E, a:a + E], w_i).then_inc(wi_full, 16)
            for k in range(CHUNKS):
                act.wait_ge(cen_ready, k + 1)
                act.activation(sq[:, tiles(k), :], cen[:, tiles(k), :], ACT.Square).then_inc(sq_ready, 1)
            act.wait_ge(var_ready, 1)
            act.activation(s2[:, :], s1[:, :], ACT.Sqrt).then_inc(std_ready, 1)
            gamma_col = gamma.rearrange("(e o) -> e o", o=1)
            for dst, src in [(gam[0:E, :], gamma_col), (gam[E:P, :], gamma_col),
                             (bet[:, :], beta.partition_broadcast(P)),
                             (wl[:, 0:E], w_l1[:, 0:E]), (wl[:, E:], w_l1[:, E:]),
                             (wl_sw[:, 0:E], w_l1[:, E:]), (wl_sw[:, E:], w_l1[:, 0:E])]:
                act.dma_start(dst, src).then_inc(late_full, 16)

            def degrees(i2, R, q0, n, first=False):
                for q in range(q0, q0 + n):
                    if not first or R:
                        done = Q * R + q - (Q - 1)
                        act.wait_ge(deg_striped, done if first else i2 * (TILES // 2) + done)
                    place = degp[:, i2 + 1, Q * R + q:Q * R + q + 1] if isinstance(i2, int) else \
                        degp[:, bass.ds(i2 + 1, 1), Q * R + q:Q * R + q + 1].rearrange("p a b -> p (a b)")
                    place_in = first_place[FIRST[R]] if first else striped[:, R % 2]
                    act.activation(junk[:, q, :], place_in[:, q, :], ACT.Copy, accum_out=place)\
                        .then_inc(deg_striped, 1)

            def to_sbuf(i, R, c, last=False):
                k = turn(R, c)
                act.wait_ge(blocks_t, i * TILES + (CC * R + c + 1))
                if c == 0 and last and R == GROUPS - 1:
                    act.wait_ge(res_ready, CHUNKS)
                elif c == 0 and R >= 2:
                    act.wait_ge(turned_used, i * GROUPS + (R - 1))
                act.copy(turned_place(R, last)[:, c, :], TA[k % 2][:, :]).then_inc(turn_full, 1)

            def superpanel(i, last=False):
                act.wait_ge(deg_striped, i * TILES + TILES)
                for R in range(GROUPS):
                    if R:
                        to_sbuf(i, R, 0, last)
                        to_sbuf(i, R, 1, last)
                    if R and not last:
                        act.wait_ge(striped_full[(R - 1) % 2], i * (16 * UNITS) + (16 * ((R - 1) // 2) + 16))
                        degrees(i * 2 + 2, R - 1, 0, 2)
                    to_sbuf(i, R, 2, last)
                    to_sbuf(i, R, 3, last)
                    if R == 0:
                        act.wait_ge(t_psum, i + 1)
                        act.copy(t_sb[:, :, :, :], TA[0][:, :].rearrange("p (c w e) -> p c w e", c=CC, w=2))\
                            .then_inc(turn_full, 1)
                    if R and not last:
                        degrees(i * 2 + 2, R - 1, 2, 2)
                    if not (last and R == GROUPS - 1):
                        if R:
                            act.wait_ge(strip_t_full, i * GROUPS + R)
                        for g in range(2, 4):
                            strips(act, g, strip_in[:, (R + 1) % 2, :, :],
                                   i * (2 * CW) + (CW if R < GROUPS - 1 else 3 * CW), SW,
                                   group_blocks((R + 1) % GROUPS)).then_inc(strip_full[(R + 1) % 2], 16)
                    if last and R == 0:
                        act.wait_ge(shared, SUPER * TILES)
                        act.wait_ge(deg_striped, SUPER * TILES)
                        for g in range(2, 4):
                            strips(act, g, last_in, 0, QUARTER, group_blocks(GROUPS - 1))\
                                .then_inc(last_full, 16)
                    if last and R % 2:
                        act.wait_ge(blocks_t, i * TILES + CC * (R + 1))
                        act.wait_ge(deg_turned, SUPER * TILES)
                        for g in range(2, 4):
                            strips(act, g, unit_in[:, R // 2, :, :], R // 2 * UW, QUARTER, group_blocks(0))\
                                .then_inc(unit_full[R // 2], 16)
                if not last:
                    act.wait_ge(striped_full[(GROUPS - 1) % 2], i * (16 * UNITS) + 16 * UNITS)
                    degrees(i * 2 + 2, GROUPS - 1, 0, Q)
                    to_sbuf(i + 1, 0, 0)
                    to_sbuf(i + 1, 0, 1)

            act.wait_ge(zeros_used, 1)
            for k in range(CHUNKS + 1):
                if k < CHUNKS:
                    act.wait_ge(h0T_psum, k + 1)
                    if k:
                        act.wait_ge(hw_psum, k)
                    act.copy(h0T[:, :, :], TA[0][:, :].rearrange("p (j r) -> p j r", j=Q)).then_inc(h0T_ready, 1)
                for R in range(2 * k - 2, 2 * k):
                    if R >= 0:
                        act.wait_ge(first_full[FIRST[R]], 16 * (FIRST[:R].count(FIRST[R]) + 1))
                        degrees(0, R, 0, Q, first=True)
            for g in range(2, 4):
                strips(act, g, strip_in[:, 0, :, :], CW, SW, group_blocks(0)).then_inc(strip_full[0], 16)
            to_sbuf(0, 0, 0)
            to_sbuf(0, 0, 1)
            with act.Fori(0, SUPER - 1) as i:
                superpanel(i)
            superpanel(SUPER - 1, last=True)
            act.wait_ge(sum_ready, 1)
            for b in range(BANKS):
                act.copy(hT[:, b, :], H[b][:, :]).then_inc(hT_ready, 1)
            for b in range(BANKS):
                act.wait_ge(hc_psum, b + 1)
                act.activation(sq[:, tiles(b), :].rearrange("p (h q) e -> p q h e", h=2),
                               mid[b][:, :].rearrange("p (q h e) -> p q h e", q=Q, h=2),
                               ACT.Square).then_inc(hsq_ready, 1)
            act.wait_ge(hvar_ready, 1)
            act.activation(s2[:, :], s1[:, :], ACT.Sqrt).then_inc(hstd_ready, 1)
            for v in range(2):
                act.wait_ge(unit_t_full, 3 + v)
                for g in range(2, 4):
                    strips(act, g, unit_in[:, v, :, :], v * UW, QUARTER, group_blocks(1)).then_inc(unit_full[v], 16)
            for b in C1_ORDER:
                if b in POOL_CHUNKS:
                    act.wait_ge(c1_pool, POOL_CHUNKS.index(b) + 1)
                else:
                    act.wait_ge(c1_ready, 1 + sum(a not in POOL_CHUNKS for a in range(b)))
                act.activation(sq[:, tiles(b), :], cen[:, tiles(b), :], ACT.Square).then_inc(c1sq_ready, 1)
            act.wait_ge(c1var_ready, 1)
            act.activation(s2[:, :], s1[:, :], ACT.Sqrt).then_inc(c1std_ready, 1)
            for a, b in F_SPANS:
                for g in range(2):
                    act.wait_ge(f_ready, (TILES // 4 * g + b - 1) // CT + 1)
                    for q in range(4):
                        cp = f_columns(act.copy, g, q, a, b)
                cp.then_inc(fcols_act, 1)

            def group_b(R, u, loads=range(UNITS), first=False):
                for v in range(UNITS):
                    if v in loads:
                        act.wait_ge(unit_t_full, R * (2 * UNITS) + 2 * (v + 1))
                    if v in loads and at(R, GROUPS - 2) and v == UNITS - 1:
                        for half in range(2):
                            for g in range(2, 4):
                                strips(act, g, half_in(half), (UNITS - 1) * UW + half * UW // 2, QUARTER,
                                       group_blocks(GROUPS - 1)).then_inc(half_full[half], 16)
                    elif v in loads:
                        for g in range(2, 4):
                            strips(act, g, unit_in[:, v, :, :], v * UW, QUARTER, group_blocks(R + 1))\
                                .then_inc(unit_full[v], 16)
                    if v == 2:
                        act.wait_ge(fT_psum, R + 1)
                        if not first:
                            act.wait_ge(out_psum, R - 1)
                        act.copy(fT[:, u, :, :], TA[0][:, 0:2 * P].rearrange("p (j r) -> p j r", j=2))\
                            .then_inc(fT_ready, 1)
                act.wait_ge(unit_used, R * UNITS + UNITS)
                act.copy(nT[:, u, :], H[u][:, :]).then_inc(nT_ready, 1)

            group_b(0, 0, loads=range(2, UNITS), first=True)
            group_b(1, 1, first=True)
            with act.Fori(1, GROUPS // 2 - 1) as it:
                group_b(it * 2, 0)
                group_b(it * 2 + 1, 1)
            group_b(GROUPS - 2, 0, loads=range(1, UNITS))
            group_b(GROUPS - 1, 1, loads=range(0))

        @block.vector
        def _(dve):
            chain = [0]

            def link(ins):
                chain[0] += 1
                ins.then_inc(dve_chain, 1)
                dve.wait_ge(dve_chain, chain[0])

            def inverse(t):
                link(dve.reciprocal(rs[:, t], s2[:, t]))
                link(dve.tensor_tensor(sn[:, t], rs[:, t], rs[:, t], ALU.mult))
                link(dve.tensor_tensor(sn[:, t], sn[:, t], s1[:, t], ALU.mult))
                link(dve.tensor_scalar(sn[:, t], sn[:, t], -0.5, 1.5, ALU.mult, ALU.add))
                link(dve.tensor_tensor(rs[:, t], rs[:, t], sn[:, t], ALU.mult))

            dve.wait_ge(ident_step, 3)
            for a in (0, HALF):
                link(dve.memset(center[a:a + HALF, a:a + HALF], -1.0 / E))
            for w in (w_user, w_item, w1T):
                dve.memset(w[0:E, E:P], 0.0)
                link(dve.memset(w[E:P, 0:E], 0.0))
            link(dve.tensor_tensor(center[:, :], center[:, :], ident[:, :], ALU.add))

            def degrees(i2, i1, R):
                dve.wait_ge(turned_full[R], i1 * 16)
                place = degp[:, i2, Q * R:Q * R + Q] if isinstance(i2, int) else \
                    degp[:, bass.ds(i2, 1), Q * R:Q * R + Q].rearrange("p j q -> p (j q)")
                dve.tensor_reduce(place, turned[:, R, :, :], AX, ALU.add).then_inc(deg_turned, Q)

            for k in range(CHUNKS):
                dve.wait_ge(x_full[k], 16)
                dve.tensor_reduce(s1[:, tiles(k)], xs[:, tiles(k), :], AX, ALU.add).then_inc(dve_chain, 1)
            chain[0] += CHUNKS
            dve.wait_ge(dve_chain, chain[0])
            link(dve.tensor_scalar(s1[:, :], s1[:, :], 1.0 / E, None, ALU.mult))
            for k in range(CHUNKS):
                dve.tensor_tensor(cen[:, tiles(k), :], xs[:, tiles(k), :], both(s1[:, tiles(k)], CT), ALU.subtract)\
                    .then_inc(cen_ready, 1)
            dve.wait_ge(cen_ready, CHUNKS)
            for k in range(CHUNKS):
                dve.wait_ge(sq_ready, k + 1)
                dve.tensor_reduce(s1[:, tiles(k)], sq[:, tiles(k), :], AX, ALU.add).then_inc(dve_chain, 1)
            chain[0] += CHUNKS
            dve.wait_ge(dve_chain, chain[0])
            dve.tensor_scalar(s1[:, :], s1[:, :], 1.0 / E, EPS, ALU.mult, ALU.add).then_inc(var_ready, 1)
            dve.wait_ge(std_ready, 1)
            inverse(slice(0, TILES))
            for k in range(CHUNKS):
                dve.scalar_tensor_tensor(h0[:, tiles(k), :], cen[:, tiles(k), :], 0.0, both(rs[:, tiles(k)], CT),
                                         ALU.max, ALU.mult).then_inc(h0_ready, 1)
                if k == 0:
                    dve.wait_ge(const_t, 1)
                    dve.wait_ge(const_full, 16 * 6)
                    link(dve.tensor_tensor(parp[:, :], par[:, 0:4:2], par[:, 1:4:2], ALU.mult))
                    NU = N_USERS // P
                    link(dve.tensor_scalar(scale[:, 0:NU], TA[0][:, 0:NU], parp[:, 0:1], None, ALU.mult))
                    dve.tensor_scalar(scale[:, NU:TILES], TA[0][:, NU:TILES], parp[:, 1:2], None, ALU.mult)\
                        .then_inc(consts_ready, 1)
            dve.wait_ge(consts_ready, 1)
            for k in range(CHUNKS):
                if k >= 2:
                    degrees(0, 1, 2 * k - 4)
                    degrees(0, 1, 2 * k - 3)
                dve.wait_ge(hw_psum, k + 1)
                link(dve.tensor_tensor(e_sb[:, tiles(k), :], TA[1][:, :].rearrange("p (t e) -> p t e", t=CT),
                                       both(scale[:, tiles(k)], CT), ALU.mult))
                dve.tensor_tensor(e_sb[:, tiles(k), :], e_sb[:, tiles(k), :], h0[:, tiles(k), :], ALU.add)\
                    .then_inc(e_ready, 1)

            def transpose_half(src, k, half):
                c = slice(half * (UC // 2), (half + 1) * (UC // 2))
                cols = slice(half * (UW // 2), (half + 1) * (UW // 2))
                dve.transpose(unit_place(k)[:, c, :].rearrange("p c (b k) -> p b c k", k=BLK),
                              src[:, :, cols].rearrange("p b (c k) -> p b c k", k=BLK)).then_inc(unit_t_full, 1)

            def transpose_unit(src, k):
                for half in range(2):
                    transpose_half(src, k, half)

            def superpanel(i, last=False):
                dve.wait_ge(shared, i * TILES + TILES)
                dve.tensor_copy(tT[0:HALF, :], TT[0:HALF, :]).then_inc(tT_ready, 1)
                dve.tensor_copy(tT[HALF:P, :].rearrange("p (c g k) -> p g c k", g=4, c=CC),
                                TT[HALF:P, :].rearrange("p (g c k) -> p g c k", g=4, c=CC)).then_inc(tT_ready, 1)
                for R in range(GROUPS):
                    dve.wait_ge(strip_full[R % 2], i * (64 * UNITS) + (64 * (R // 2) + 64))
                    if R >= 2 and not (last and R >= GROUPS - 2):
                        dve.wait_ge(strip_used, i * GROUPS + (R - 1))
                    dve.transpose(strip_place(R, last).rearrange("p c (b k) -> p b c k", k=BLK),
                                  strip_in[:, R % 2, :, :].rearrange("p b (c k) -> p b c k", k=BLK))\
                        .then_inc(strip_t_full, 1)
                    if R and not last:
                        degrees(i * 2 + 2, i + 2, R - 1)
                    if last and R == 1:
                        dve.wait_ge(deg_turned, SUPER * TILES)
                        dve.wait_ge(deg_striped, SUPER * TILES)
                        link(dve.tensor_reduce(rdeg[:, :], degp[:, :, :].rearrange("p j c -> p c j"), AX, ALU.add))
                        link(dve.tensor_scalar(rdeg[:, :], rdeg[:, :], 1.0, None, ALU.add))
                        link(dve.reciprocal(rdeg[:, :], rdeg[:, :]))
                    if last and R == 3:
                        for k in range(CHUNKS):
                            dve.wait_ge(res_ready, k + 1)
                            dve.tensor_reduce(res_mean[:, tiles(k)], res[:, tiles(k), :], AX, ALU.add)\
                                .then_inc(dve_chain, 1)
                        chain[0] += CHUNKS
                        dve.wait_ge(dve_chain, chain[0])
                        link(dve.tensor_scalar(res_mean[:, :], res_mean[:, :], 1.0 / E, None, ALU.mult))
                        for k in range(CHUNKS):
                            dve.tensor_tensor(res[:, tiles(k), :], res[:, tiles(k), :], both(res_mean[:, tiles(k)], CT),
                                              ALU.subtract).then_inc(res_mid, 1)
                    if last and R == GROUPS - 2:
                        dve.wait_ge(unit_full[0], 64)
                        dve.wait_ge(turned_used, SUPER * GROUPS - 2)
                        transpose_half(unit_in[:, 0, :, :], 0, 1)
                        dve.wait_ge(unit_full[1], 64)
                        dve.wait_ge(strip_used, SUPER * GROUPS - 3)
                        transpose_half(unit_in[:, 1, :, :], 1, 0)
                if not last:
                    degrees(i * 2 + 2, i + 2, GROUPS - 1)

            dve.wait_ge(late_full, 16 * 7)
            link(dve.memset(gam_center[:, P:P + 2], 0.0))
            link(dve.tensor_scalar(gam_center[:, 0:P], center[:, :], gam[:, 0:1], None, ALU.mult))
            link(dve.tensor_scalar(gam_center[0:E, P:P + 1], gam[0:E, :], 1.0 / E, None, ALU.mult))
            dve.tensor_scalar(gam_center[E:P, P + 1:P + 2], gam[E:P, :], 1.0 / E, None, ALU.mult).then_inc(gam_ready, 1)
            degrees(0, 1, 2 * CHUNKS - 4)
            degrees(0, 1, 2 * CHUNKS - 3)
            dve.wait_ge(late_t, 1)
            link(dve.tensor_copy(w1T[0:E, 0:E], TA[0][0:E, 0:64]))
            link(dve.tensor_copy(w1T[E:P, E:P], TA[0][E:P, 64:128]))
            link(dve.tensor_copy(w2T[0:E, :], TA[0][0:E, 64:128]))
            link(dve.tensor_copy(w2T[E:P, :], TA[0][E:P, 0:64]))
            dve.tensor_copy(turn_center[:, :], TA[1][:, 0:P + 2]).then_inc(late_ready, 1)
            for R in range(2 * CHUNKS - 2, GROUPS):
                degrees(0, 1, R)
            with dve.Fori(0, SUPER - 1) as i:
                superpanel(i)
            superpanel(SUPER - 1, last=True)

            dve.wait_ge(turned_used, SUPER * GROUPS - 1)
            transpose_half(unit_in[:, 0, :, :], 0, 0)
            dve.wait_ge(strip_used, SUPER * GROUPS - 2)
            transpose_half(unit_in[:, 1, :, :], 1, 1)

            for b in range(BANKS):
                dve.wait_ge(hsq_ready, b + 1)
                dve.tensor_reduce(s1[:, tiles(b)], sq[:, tiles(b), :], AX, ALU.add).then_inc(dve_chain, 1)
            chain[0] += BANKS
            dve.wait_ge(dve_chain, chain[0])
            dve.tensor_scalar(s1[:, :], s1[:, :], 1.0 / E, EPS, ALU.mult, ALU.add).then_inc(hvar_ready, 1)
            dve.wait_ge(hstd_ready, 1)
            inverse(slice(0, TILES))
            dve.wait_ge(res_mid, CHUNKS)
            for b in range(BANKS):
                dve.wait_ge(gc_psum, b + 1)
                for h in range(2):
                    th = slice(CT * b + Q * h, CT * b + Q * h + Q)
                    dve.tensor_tensor(cen[:, th, :], midg[b][:, :].rearrange("p (q h e) -> p h q e", q=Q, h=2)[:, h],
                                      both(rs[:, th], Q), ALU.mult).then_inc(cr_ready, 1)
                if b not in POOL_CHUNKS:
                    dve.wait_ge(cr_ready, 2 * b + 2)
                    dve.tensor_tensor(cen[:, tiles(b), :], cen[:, tiles(b), :], res[:, tiles(b), :], ALU.add)\
                        .then_inc(c1_ready, 1)
            dve.wait_ge(cr_ready, 2 * BANKS)
            for n, b in enumerate(C1_ORDER):
                dve.wait_ge(c1sq_ready, n + 1)
                dve.tensor_reduce(s1[:, tiles(b)], sq[:, tiles(b), :], AX, ALU.add).then_inc(dve_chain, 1)
            chain[0] += BANKS
            dve.wait_ge(dve_chain, chain[0])
            dve.tensor_scalar(s1[:, :], s1[:, :], 1.0 / E, EPS, ALU.mult, ALU.add).then_inc(c1var_ready, 1)
            dve.wait_ge(mean_psum, 1)
            link(dve.tensor_tensor(x1_mean[:, :].rearrange("p (b h q) -> p b h q", b=BANKS, h=2),
                                   TT[:, 0:2 * BANKS * Q].rearrange("p (b q h) -> p b h q", b=BANKS, h=2),
                                   rs[:, :].rearrange("p (b h q) -> p b h q", b=BANKS, h=2), ALU.mult))
            dve.tensor_tensor(x1_mean[:, :], x1_mean[:, :], res_mean[:, :], ALU.add).then_inc(x1_mean_ready, 1)
            dve.wait_ge(x1_mean_ready, 1)
            dve.wait_ge(c1std_ready, 1)
            inverse(slice(0, TILES))
            for b in range(BANKS):
                t = tiles(b)
                dve.scalar_tensor_tensor(f_sb[:, t, :], cen[:, t, :], 0.0, both(rs[:, t], CT), ALU.max,
                                         ALU.mult).then_inc(f_ready, 1)
            dve.wait_ge(f_ready, CHUNKS)
            for g in range(2, 4):
                for q in range(4):
                    cp = f_columns(dve.tensor_copy, g, q, *F_SPANS[0])
            cp.then_inc(fcols_dve, 1)

            def group_out(R1, R_half, u, first=False):
                cols = TA[1][:, :].rearrange("p (w q e) -> p w q e", q=Q, w=2)
                dve.wait_ge(out_psum, R1)
                if not at(R1, 1):
                    dve.wait_ge(obuf_ready, R1 - 1)
                t = slice(Q * R1 - Q, Q * R1) if isinstance(R1, int) else bass.ds(R1 * Q - Q, Q)
                dve.tensor_tensor(o1[:, :, :], cols[:, 1, :, :], both(rdeg[:, t], Q), ALU.mult)\
                    .then_inc(o1_ready, 1)
                dve.tensor_tensor(o2[:, :, :], cols[:, 0, :, :], xs[:, t, :], ALU.add).then_inc(o2_ready, 1)
                dve.wait_ge(o1_ready, R1)
                dve.wait_ge(o2_ready, R1)
                if not first:
                    dve.wait_ge(stored[u], R_half * 16)
                dve.tensor_tensor(obuf[:, u, :, :], o1[:, :, :], o2[:, :, :], ALU.add).then_inc(obuf_ready, 1)

            def units_ahead(R, u, loads, frm=0, upto=UNITS):
                for w in range(2 + frm, 2 + upto):
                    resident = at(R, GROUPS - 2) and w == UNITS
                    final = at(R, GROUPS - 1) and w == UNITS - 1
                    if resident:
                        dve.wait_ge(last_full, 64)
                    elif not final:
                        dve.wait_ge(unit_full[w % UNITS], loads + w // UNITS * 64)
                    place = UNITS * u + w + (0 if at(R, 0) or at(R, 1) else 2 * UNITS)
                    if place > 4:
                        dve.wait_ge(unit_used, R * UNITS + (w - 1))
                    elif place > 2:
                        dve.wait_ge(unit_used, w - 2)
                    if final:
                        for half in range(2):
                            dve.wait_ge(half_full[half], 64)
                            transpose_half(unit_in[:, w % UNITS, :, :], place, half)
                    else:
                        transpose_unit(last_in if resident else unit_in[:, w % UNITS, :, :], place)

            dve.wait_ge(mean_psum, 1)
            dve.wait_ge(c1_pool, len(POOL_CHUNKS))
            dve.wait_ge(c1_ready, BANKS - len(POOL_CHUNKS))
            units_ahead(0, 0, 64, upto=1)
            for g in range(2, 4):
                for q in range(4):
                    cp = f_columns(dve.tensor_copy, g, q, *F_SPANS[1])
            cp.then_inc(fcols_dve, 1)
            units_ahead(0, 0, 64, frm=1)
            units_ahead(1, 1, 128)
            group_out(1, 0, 0, first=True)
            units_ahead(2, 0, 192)
            group_out(2, 0, 1, first=True)
            with dve.Fori(1, GROUPS // 2 - 2) as it:
                units_ahead(it * 2 + 1, 1, it * 128 + 128)
                group_out(it * 2 + 1, it, 0)
                units_ahead(it * 2 + 2, 0, it * 128 + 192)
                group_out(it * 2 + 2, it, 1)
            for R in range(GROUPS - 3, GROUPS):
                units_ahead(R, R % 2, 64 * (R + 1), upto=UNITS if R < GROUPS - 1 else UNITS - 2)
                group_out(R, (R - 1) // 2, (R - 1) % 2)
            group_out(GROUPS, GROUPS // 2 - 1, 1)


_INS = ['x', 'adj', 'L0_gnn_W_u', 'L0_gnn_diag_u', 'L0_gnn_par_u', 'L0_gnn_W_i', 'L0_gnn_diag_i',
        'L0_gnn_par_i', 'L0_gnn_ln_gamma', 'L0_gnn_ln_beta', 'L1_gnn_W']
_OUTS = [((5120, 64), 'float32')]


def kernel(**inputs):
    import numpy as _np
    import concourse.bacc as _bacc
    from concourse import mybir as _mybir
    from concourse.bass_utils import run_bass_kernel_spmd as _run

    nc = _bacc.Bacc("TRN2", target_bir_lowering=False, num_devices=1)
    arrays, args = {}, []
    for name in _INS:
        a = _np.ascontiguousarray(inputs[name])
        arrays[f"in_{name}_dram"] = a
        args.append(nc.dram_tensor(f"in_{name}_dram", a.shape, _mybir.dt.from_np(a.dtype), kind="ExternalInput").ap())
    for i, (shape, dtype) in enumerate(_OUTS):
        dt = _mybir.dt.from_np(_np.dtype(dtype))
        args.append(nc.dram_tensor(f"out_{i}_dram", shape, dt, kind="ExternalOutput").ap())
    gnn_kernel(nc, *args)
    r = _run(nc, [arrays], core_ids=[0])
    got = tuple(r.results[0][f"out_{i}_dram"] for i in range(len(_OUTS)))
    return got[0]
```
